# Optimizing a Trainium2 kernel written in Bass

```python
import numpy as np
import jax
import jax.numpy as jnp

def _softmax(x, axis=-1):
    return jax.nn.softmax(x, axis=axis)

def _gelu(x):
    return jax.nn.gelu(x, approximate=True)

def _silu(x):
    return jax.nn.silu(x)

def _sigmoid(x):
    return jax.nn.sigmoid(x)

def _layernorm(x, axis=-1, eps=1e-05):
    m = jnp.mean(x, axis=axis, keepdims=True)
    v = jnp.var(x, axis=axis, keepdims=True)
    return (x - m) / jnp.sqrt(v + eps)

def _scatter_add(tgt, idx, src, axis=0):
    return tgt.at[idx].add(src)

def _segment_sum(src, seg, n):
    return jax.ops.segment_sum(src, seg, n)
kernel_name = 'mk_gnn_ffn_d1_gnn_r8_4f9b85'

def setup_inputs(seed: int=0):
    np.random.seed(seed)
    _w = jnp.asarray

    def _rec_inputs():
        import jax
        import jax.numpy as jnp
        _gk = jax.random.key(seed)
        x = -0.0003713 + 1 * jax.random.normal(jax.random.fold_in(_gk, 1), (6250, 256), jnp.float32)
        src = jax.random.randint(jax.random.fold_in(_gk, 2), (200000,), 0, 6250, jnp.int32)
        dst = jax.random.randint(jax.random.fold_in(_gk, 3), (200000,), 0, 6250, jnp.int32)
        _o = jnp.argsort(dst, stable=True)
        src = src[_o]
        dst = dst[_o]
        return (x, src, dst)
    x, src, dst = _rec_inputs()

    def _L0_gnn_setup():
        import jax, jax.numpy as jnp
        import numpy as np
        N, HID, HEADS = (6250, 256, 8)
        D = HID // HEADS
        E = 100000

        def _gnn_layer(x, edge_index, Wq, bq, Wk, bk, Wv, bv, Wskip, bskip, gamma, beta):
            n = x.shape[0]
            src, dst = (edge_index[0], edge_index[1])
            q = (x @ Wq + bq).reshape(n, HEADS, D)
            k = (x @ Wk + bk).reshape(n, HEADS, D)
            v = (x @ Wv + bv).reshape(n, HEADS, D)
            logits = jnp.einsum('ehd,ehd->eh', q[dst], k[src]) / jnp.sqrt(jnp.float32(D))
            seg_max = jax.ops.segment_max(logits, dst, num_segments=n)
            expv = jnp.exp(logits - seg_max[dst])
            denom = jax.ops.segment_sum(expv, dst, num_segments=n)
            attn = expv / denom[dst]
            agg = jax.ops.segment_sum(attn[:, :, None] * v[src], dst, num_segments=n)
            out = agg.reshape(n, HID) + (x @ Wskip + bskip)
            h = jax.nn.gelu(out, approximate=False)
            y = x + h
            mu = jnp.mean(y, axis=-1, keepdims=True)
            var = jnp.var(y, axis=-1, keepdims=True)
            return (y - mu) / jnp.sqrt(var + 1e-05) * gamma + beta
        key = jax.random.key(seed)
        ks = jax.random.split(key, 12)
        s = 0.02
        x = jax.random.normal(ks[0], (N, HID), dtype=jnp.float32)
        edge_index = jax.random.randint(ks[1], (2, E), 0, N, dtype=jnp.int64)
        Wq = jax.random.normal(ks[2], (HID, HID), dtype=jnp.float32) * s
        bq = jnp.zeros((HID,), dtype=jnp.float32)
        Wk = jax.random.normal(ks[3], (HID, HID), dtype=jnp.float32) * s
        bk = jnp.zeros((HID,), dtype=jnp.float32)
        Wv = jax.random.normal(ks[4], (HID, HID), dtype=jnp.float32) * s
        bv = jnp.zeros((HID,), dtype=jnp.float32)
        Wskip = jax.random.normal(ks[5], (HID, HID), dtype=jnp.float32) * s
        bskip = jnp.zeros((HID,), dtype=jnp.float32)
        gamma = jnp.ones((HID,), dtype=jnp.float32)
        beta = jnp.zeros((HID,), dtype=jnp.float32)
        return {'x': x, 'edge_index': edge_index, 'Wq': Wq, 'bq': bq, 'Wk': Wk, 'bk': bk, 'Wv': Wv, 'bv': bv, 'Wskip': Wskip, 'bskip': bskip, 'gamma': gamma, 'beta': beta}
    _L0_gnn_all = _L0_gnn_setup()
    _L0_gnn_in = {k: v for k, v in _L0_gnn_all.items() if k in ('Wq', 'bq', 'Wk', 'bk', 'Wv', 'bv', 'Wskip', 'bskip', 'gamma', 'beta')}
    del _L0_gnn_all

    def _L0_ffn_setup():
        import jax, jax.numpy as jnp
        import numpy as np
        B, N, D = (16, 512, 256)
        NUM_EXPERTS, TOP_K, HEADS = (4, 2, 4)
        N_EDGES = 131072
        LN_EPS = 1e-05

        def _layernorm(x, g, b):
            mu = x.mean(-1, keepdims=True)
            var = ((x - mu) ** 2).mean(-1, keepdims=True)
            return (x - mu) * jax.lax.rsqrt(var + LN_EPS) * g + b

        def _forward(x, edge_index, W_gat, att_src, att_dst, b_gat, ln_gamma, ln_beta, W1, b1, W2, b2):
            Bc, Nc, Dc = x.shape
            M = Bc * Nc
            x_flat = x.reshape(M, Dc)
            h = (x_flat @ W_gat).reshape(M, HEADS, NUM_EXPERTS)
            loops = jnp.arange(M, dtype=edge_index.dtype)
            src = jnp.concatenate([edge_index[0], loops])
            dst = jnp.concatenate([edge_index[1], loops])
            a_src = (h * att_src).sum(-1)
            a_dst = (h * att_dst).sum(-1)
            e = jax.nn.leaky_relu(a_src[src] + a_dst[dst], negative_slope=0.2)
            e_max = jax.ops.segment_max(e, dst, num_segments=M)
            ee = jnp.exp(e - e_max[dst])
            denom = jax.ops.segment_sum(ee, dst, num_segments=M)
            alpha = ee / (denom[dst] + 1e-16)
            msg = h[src] * alpha[:, :, None]
            agg = jax.ops.segment_sum(msg, dst, num_segments=M).reshape(M, HEADS * NUM_EXPERTS) + b_gat
            scores = _layernorm(agg, ln_gamma, ln_beta).reshape(M, HEADS, NUM_EXPERTS).mean(1)
            scores = scores.reshape(Bc, Nc, NUM_EXPERTS)
            topk_s, topk_i = jax.lax.top_k(scores, TOP_K)
            w = jax.nn.softmax(topk_s, axis=-1)
            out = jnp.zeros_like(x)
            for ei in range(NUM_EXPERTS):
                g = jnp.where(topk_i == ei, w, 0.0).sum(-1)
                hh = jax.nn.gelu(x @ W1[ei] + b1[ei], approximate=False)
                out = out + g[..., None] * (hh @ W2[ei] + b2[ei])
            return out
        key = jax.random.key(seed)
        ks = jax.random.split(key, 8)
        s = 0.05
        return {'x': jax.random.normal(ks[0], (B, N, D), jnp.float32), 'W_gat': jax.random.normal(ks[1], (D, HEADS * NUM_EXPERTS), jnp.float32) * s, 'att_src': jax.random.normal(ks[2], (HEADS, NUM_EXPERTS), jnp.float32) * s, 'att_dst': jax.random.normal(ks[3], (HEADS, NUM_EXPERTS), jnp.float32) * s, 'b_gat': jnp.zeros((HEADS * NUM_EXPERTS,), jnp.float32), 'ln_gamma': jnp.ones((HEADS * NUM_EXPERTS,), jnp.float32), 'ln_beta': jnp.zeros((HEADS * NUM_EXPERTS,), jnp.float32), 'W1': jax.random.normal(ks[4], (NUM_EXPERTS, D, 2 * D), jnp.float32) * s, 'b1': jnp.zeros((NUM_EXPERTS, 2 * D), jnp.float32), 'W2': jax.random.normal(ks[5], (NUM_EXPERTS, 2 * D, D), jnp.float32) * s, 'b2': jnp.zeros((NUM_EXPERTS, D), jnp.float32), 'edge_index': jax.random.randint(ks[6], (2, N_EDGES), 0, B * N, jnp.int32)}
    _L0_ffn_all = _L0_ffn_setup()
    _L0_ffn_in = {k: v for k, v in _L0_ffn_all.items() if k in ('W_gat', 'att_src', 'att_dst', 'b_gat', 'ln_gamma', 'ln_beta', 'W1', 'b1', 'W2', 'b2', 'edge_index')}
    del _L0_ffn_all
    return {'x': x, 'src': src, 'dst': dst, 'L0_gnn_Wq': _L0_gnn_in['Wq'], 'L0_gnn_bq': _L0_gnn_in['bq'], 'L0_gnn_Wk': _L0_gnn_in['Wk'], 'L0_gnn_bk': _L0_gnn_in['bk'], 'L0_gnn_Wv': _L0_gnn_in['Wv'], 'L0_gnn_bv': _L0_gnn_in['bv'], 'L0_gnn_Wskip': _L0_gnn_in['Wskip'], 'L0_gnn_bskip': _L0_gnn_in['bskip'], 'L0_gnn_gamma': _L0_gnn_in['gamma'], 'L0_gnn_beta': _L0_gnn_in['beta'], 'L0_ffn_W_gat': _L0_ffn_in['W_gat'], 'L0_ffn_att_src': _L0_ffn_in['att_src'], 'L0_ffn_att_dst': _L0_ffn_in['att_dst'], 'L0_ffn_b_gat': _L0_ffn_in['b_gat'], 'L0_ffn_ln_gamma': _L0_ffn_in['ln_gamma'], 'L0_ffn_ln_beta': _L0_ffn_in['ln_beta'], 'L0_ffn_W1': _L0_ffn_in['W1'], 'L0_ffn_b1': _L0_ffn_in['b1'], 'L0_ffn_W2': _L0_ffn_in['W2'], 'L0_ffn_b2': _L0_ffn_in['b2'], 'L0_ffn_edge_index': _L0_ffn_in['edge_index']}

def reference(x, src, dst, L0_gnn_Wq, L0_gnn_bq, L0_gnn_Wk, L0_gnn_bk, L0_gnn_Wv, L0_gnn_bv, L0_gnn_Wskip, L0_gnn_bskip, L0_gnn_gamma, L0_gnn_beta, L0_ffn_W_gat, L0_ffn_att_src, L0_ffn_att_dst, L0_ffn_b_gat, L0_ffn_ln_gamma, L0_ffn_ln_beta, L0_ffn_W1, L0_ffn_b1, L0_ffn_W2, L0_ffn_b2, L0_ffn_edge_index):
    import jax
    import jax.numpy as jnp

    def _L0_gnn_ref(x, edge_index, Wq, bq, Wk, bk, Wv, bv, Wskip, bskip, gamma, beta):
        import jax, jax.numpy as jnp
        import numpy as np
        N, HID, HEADS = (6250, 256, 8)
        D = HID // HEADS
        E = 100000

        def _gnn_layer(x, edge_index, Wq, bq, Wk, bk, Wv, bv, Wskip, bskip, gamma, beta):
            n = x.shape[0]
            src, dst = (edge_index[0], edge_index[1])
            q = (x @ Wq + bq).reshape(n, HEADS, D)
            k = (x @ Wk + bk).reshape(n, HEADS, D)
            v = (x @ Wv + bv).reshape(n, HEADS, D)
            logits = jnp.einsum('ehd,ehd->eh', q[dst], k[src]) / jnp.sqrt(jnp.float32(D))
            seg_max = jax.ops.segment_max(logits, dst, num_segments=n)
            expv = jnp.exp(logits - seg_max[dst])
            denom = jax.ops.segment_sum(expv, dst, num_segments=n)
            attn = expv / denom[dst]
            agg = jax.ops.segment_sum(attn[:, :, None] * v[src], dst, num_segments=n)
            out = agg.reshape(n, HID) + (x @ Wskip + bskip)
            h = jax.nn.gelu(out, approximate=False)
            y = x + h
            mu = jnp.mean(y, axis=-1, keepdims=True)
            var = jnp.var(y, axis=-1, keepdims=True)
            return (y - mu) / jnp.sqrt(var + 1e-05) * gamma + beta
        return _gnn_layer(x, edge_index, Wq, bq, Wk, bk, Wv, bv, Wskip, bskip, gamma, beta)

    def _L0_ffn_ref(x, W_gat, att_src, att_dst, b_gat, ln_gamma, ln_beta, W1, b1, W2, b2, edge_index):
        import jax, jax.numpy as jnp
        import numpy as np
        B, N, D = (16, 512, 256)
        NUM_EXPERTS, TOP_K, HEADS = (4, 2, 4)
        N_EDGES = 131072
        LN_EPS = 1e-05

        def _layernorm(x, g, b):
            mu = x.mean(-1, keepdims=True)
            var = ((x - mu) ** 2).mean(-1, keepdims=True)
            return (x - mu) * jax.lax.rsqrt(var + LN_EPS) * g + b

        def _forward(x, edge_index, W_gat, att_src, att_dst, b_gat, ln_gamma, ln_beta, W1, b1, W2, b2):
            Bc, Nc, Dc = x.shape
            M = Bc * Nc
            x_flat = x.reshape(M, Dc)
            h = (x_flat @ W_gat).reshape(M, HEADS, NUM_EXPERTS)
            loops = jnp.arange(M, dtype=edge_index.dtype)
            src = jnp.concatenate([edge_index[0], loops])
            dst = jnp.concatenate([edge_index[1], loops])
            a_src = (h * att_src).sum(-1)
            a_dst = (h * att_dst).sum(-1)
            e = jax.nn.leaky_relu(a_src[src] + a_dst[dst], negative_slope=0.2)
            e_max = jax.ops.segment_max(e, dst, num_segments=M)
            ee = jnp.exp(e - e_max[dst])
            denom = jax.ops.segment_sum(ee, dst, num_segments=M)
            alpha = ee / (denom[dst] + 1e-16)
            msg = h[src] * alpha[:, :, None]
            agg = jax.ops.segment_sum(msg, dst, num_segments=M).reshape(M, HEADS * NUM_EXPERTS) + b_gat
            scores = _layernorm(agg, ln_gamma, ln_beta).reshape(M, HEADS, NUM_EXPERTS).mean(1)
            scores = scores.reshape(Bc, Nc, NUM_EXPERTS)
            topk_s, topk_i = jax.lax.top_k(scores, TOP_K)
            w = jax.nn.softmax(topk_s, axis=-1)
            out = jnp.zeros_like(x)
            for ei in range(NUM_EXPERTS):
                g = jnp.where(topk_i == ei, w, 0.0).sum(-1)
                hh = jax.nn.gelu(x @ W1[ei] + b1[ei], approximate=False)
                out = out + g[..., None] * (hh @ W2[ei] + b2[ei])
            return out
        return _forward(x, edge_index, W_gat, att_src, att_dst, b_gat, ln_gamma, ln_beta, W1, b1, W2, b2)
    edge_index = jnp.stack([src, dst])
    x = x + _L0_gnn_ref(_layernorm(x, axis=-1), edge_index, L0_gnn_Wq, L0_gnn_bq, L0_gnn_Wk, L0_gnn_bk, L0_gnn_Wv, L0_gnn_bv, L0_gnn_Wskip, L0_gnn_bskip, L0_gnn_gamma, L0_gnn_beta)
    x = x + _L0_ffn_ref(_layernorm(x, axis=-1)[None], L0_ffn_W_gat, L0_ffn_att_src, L0_ffn_att_dst, L0_ffn_b_gat, L0_ffn_ln_gamma, L0_ffn_ln_beta, L0_ffn_W1, L0_ffn_b1, L0_ffn_W2, L0_ffn_b2, L0_ffn_edge_index)[0]
    return x

_drawn_inputs = setup_inputs


def setup_inputs(seed=0):
    import zlib

    import numpy as np

    out = dict(_drawn_inputs(seed))
    spreads = {'L0_gnn_bq': (0.0, 0.8),
     'L0_gnn_bk': (0.0, 0.8),
     'L0_gnn_bv': (0.0, 0.1),
     'L0_gnn_bskip': (0.0, 0.1),
     'L0_gnn_gamma': (1.0, 0.2),
     'L0_gnn_beta': (0.0, 0.1),
     'L0_ffn_b_gat': (0.0, 0.1),
     'L0_ffn_ln_gamma': (1.0, 0.2),
     'L0_ffn_ln_beta': (0.0, 0.1),
     'L0_ffn_b1': (0.0, 0.298),
     'L0_ffn_b2': (0.0, 0.1)}
    factors = {'L0_gnn_Wq': 8.0, 'L0_gnn_Wk': 8.0, 'L0_gnn_Wv': 2.698, 'L0_ffn_att_dst': 4.15}
    for name, (base, spread) in spreads.items():
        noise = np.random.default_rng([zlib.crc32(name.encode()), seed]).standard_normal(out[name].shape)
        drawn = base * np.exp(spread * noise) if base else spread * noise
        out[name] = jnp.asarray(drawn.astype(out[name].dtype))
    for name, factor in factors.items():
        out[name] = (out[name] * factor).astype(out[name].dtype)
    return out
```

```python
from contextlib import ExitStack

import concourse.bass as bass
from concourse import mybir

F32 = mybir.dt.float32
I32 = mybir.dt.int32
BF16 = mybir.dt.bfloat16
F16 = mybir.dt.float16
ALU = mybir.AluOpType
ACT = mybir.ActivationFunctionType
AX = mybir.AxisListType

P = 128
N, D = 6250, 256
NW = -(-N // P)
NPAD = NW * P
TAIL = N - (NW - 1) * P
HEADS = 8
DH = D // HEADS
HW = DH + 1
E = 200000
G = 4
NG = -(-E // (G * P))
NT = NG * G
KROW = -(-NT // P)
STEPS = NG + NW - 1
LOOP = 4
RUN = 1 + LOOP * (-(-(STEPS - 1) // LOOP))
NS = RUN + 3
TG = G * HEADS
BIG = float(2.0 ** 100)
SCALE = float(DH) ** -0.5
EPS = 1e-5
PAD_DST = 8192

RE = 131072
RH, NE = 4, 4
RD = RH * NE
RV = RD + RH
RT = RE // P
RG = 8
RSTEPS = RT // RG
BLK = 6
SPAN = -(-N // BLK)
CH = 348
FF = 512
CW = 7
NB = NW // CW
CN = CW * P


class Count:

    def __init__(self, sem):
        self.sem, self.n = sem, 0

    def on(self, ins, by=1):
        self.n += by
        return ins.then_inc(self.sem, by)


def bc(ap, shape):
    return ap.broadcast_to(shape)


def edge_tables(nc, k, src, dst):
    with ExitStack() as ctx:
        sb = lambda n, s, d: ctx.enter_context(nc.sbuf_tensor(n, s, d))
        src_row = sb("src_row", [P, KROW, P], I32)
        dst_row = sb("dst_row", [P, KROW, P], I32)
        srcf_row = sb("srcf_row", [P, KROW, P], F32)
        dstf_row = sb("dstf_row", [P, KROW, P], F32)
        last_row = sb("last_row", [P, KROW, P], F32)
        reset_row = sb("reset_row", [P, KROW, P], F32)
        differs = sb("differs", [P, KROW, P - 1], F32)
        ends = sb("ends", [P, P], F32)
        threshold = sb("threshold", [P, 1], F32)
        part = sb("part", [P, 1], F32)
        steps = sb("steps", [P, NS], F32)
        below = sb("below", [P, NG], F32)
        event = sb("event", [P, 2], F32)
        passed = sb("passed", [P, NS], F32)
        ones = sb("ones", [P, P], F32)
        wstep = sb("wstep", [P, NS], F32)
        gstep = sb("gstep", [P, NS], F32)
        bank = [ctx.enter_context(nc.psum_tensor(f"et{i}", [P, 512], F32)) for i in range(4)]
        padded, landed, dve, turned, evac, stored, made, mm = (
            nc.alloc_semaphore(n) for n in ("et_padded", "et_landed", "et_dve", "et_turned", "et_evacuated",
                                            "et_stored", "et_constants", "et_products"))
        full = E // P - P * (KROW - 1)
        rest = E % P
        e0 = P * P * (KROW - 1)
        with nc.Block() as block:
            @block.sync
            def _(sp):
                for a, row in ((src, src_row), (dst, dst_row)):
                    sp.dma_start(row[:, 0:KROW - 1, :], a[0:e0].rearrange("(k r p) -> r k p", r=P, p=P)).then_inc(landed, 16)
                sp.wait_ge(padded, 2)
                for a, row in ((src, src_row), (dst, dst_row)):
                    sp.dma_start(row[0:full, KROW - 1, :], a[e0:e0 + full * P].rearrange("(r p) -> r p", p=P)).then_inc(landed, 16)
                    sp.dma_start(row[full:full + 1, KROW - 1, 0:rest], a[e0 + full * P:E].rearrange("(r p) -> r p", r=1)).then_inc(landed, 16)
                sp.wait_ge(dve, 6)
                for b in range(KROW):
                    sp.dma_start(k.reset_d[P * b:P * (b + 1), :, :], bc(reset_row[:, b:b + 1, :], [P, HEADS, P])).then_inc(stored, 16)
                sp.wait_ge(stored, 16 * KROW)

            @block.gpsimd
            def _(pool):
                pool.memset(k.ident[:, :], 0.0).then_inc(made, 1)
                pool.memset(ones[:, :], 1.0).then_inc(made, 1)
                pool.memset(k.negbig[:, :], -BIG / P).then_inc(made, 1)
                pool.memset(k.ones_b[:, :], 1.0).then_inc(made, 1)
                pool.iota(k.iota_b[:, :], [[1, P]], base=0, channel_multiplier=0, allow_small_or_imprecise_dtypes=True).then_inc(made, 1)
                pool.iota(threshold[:, :], [[0, 1]], base=P, channel_multiplier=P, allow_small_or_imprecise_dtypes=True).then_inc(made, 1)
                pool.iota(part[:, :], [[0, 1]], base=0, channel_multiplier=1, allow_small_or_imprecise_dtypes=True).then_inc(made, 1)
                pool.iota(steps[:, :], [[1, NS]], base=0, channel_multiplier=0, allow_small_or_imprecise_dtypes=True).then_inc(made, 1)
                pool.wait_ge(made, 8)
                pool.affine_select(out=k.ident[:, :], in_=k.ident[:, :], compare_op=ALU.not_equal, fill=1.0,
                                   base=0, pattern=[[-1, P]], channel_multiplier=1).then_inc(made, 1)

            @block.vector
            def _(v):
                d = Count(dve)
                v.memset(src_row[:, KROW - 1, :], 0).then_inc(padded, 1)
                v.memset(dst_row[:, KROW - 1, :], PAD_DST).then_inc(padded, 1)
                v.wait_ge(landed, 96)
                d.on(v.tensor_copy(dstf_row[:, :, :], dst_row[:, :, :]))
                d.on(v.tensor_copy(srcf_row[:, :, :], src_row[:, :, :]))
                v.wait_ge(dve, 1)
                d.on(v.tensor_tensor(differs[:, :, :], dstf_row[:, :, 0:P - 1], dstf_row[:, :, 1:P], ALU.not_equal))
                d.on(v.memset(reset_row[:, :, 0:1], 0.0))
                d.on(v.memset(last_row[:, :, P - 1:P], BIG))
                v.wait_ge(dve, 3)
                d.on(v.tensor_scalar(reset_row[:, :, 1:P], differs[:, :, :], -BIG, None, ALU.mult))
                d.on(v.tensor_scalar(last_row[:, :, 0:P - 1], differs[:, :, :], BIG, None, ALU.mult))
                v.wait_ge(made, 9)
                v.tensor_copy(k.ident_b[:, :], k.ident[:, :]).then_inc(made, 1)
                d.on(v.tensor_copy(ends[:, :], bc(k.ident[:, P - 1:P], [P, P])))
                for b in range(KROW):
                    n = min(P, NT - P * b)
                    at = slice(P * b, P * b + n)
                    ps = bank[b % 2]
                    v.wait_ge(turned, b + 1)
                    v.tensor_copy(k.src_i[:, at], ps[:, 0:n])
                    v.tensor_copy(k.dst_f[:, at], ps[:, P:P + n])
                    v.tensor_copy(k.last_b[:, at], ps[:, 2 * P:2 * P + n]).then_inc(evac, 1)
                v.wait_ge(mm, 1)
                d.on(v.tensor_scalar(below[:, :], bank[2][:, 0:NG], threshold[:, :], None, ALU.is_lt))
                v.wait_ge(dve, d.n)
                d.on(v.reduce_sum(event[:, 0:1], below[:, :], AX.X))
                v.wait_ge(dve, d.n)
                d.on(v.tensor_tensor(event[:, 1:2], event[:, 0:1], part[:, :], ALU.add))
                v.wait_ge(dve, d.n)
                d.on(v.tensor_scalar(passed[:, :], steps[:, :], event[:, 1:2], None, ALU.is_gt))
                v.wait_ge(mm, 2)
                d.on(v.tensor_scalar(wstep[:, :], bank[3][:, 0:NS], float(NW - 1), None, ALU.min))
                v.wait_ge(dve, d.n)
                d.on(v.tensor_tensor(gstep[:, :], steps[:, :], wstep[:, :], ALU.subtract))
                d.on(v.tensor_scalar(k.wbase[:, :], wstep[:, :], float(P), None, ALU.mult))
                v.wait_ge(dve, d.n)
                d.on(v.memset(k.wbase[:, STEPS:NS], 1.0e6))
                v.tensor_copy(k.w_tab[:, :], wstep[0:1, :])
                d.on(v.tensor_scalar(k.g_tab[:, :], gstep[0:1, :], float(NG - 1), float(G), ALU.min, ALU.mult))

            @block.tensor
            def _(pe):
                pe.wait_ge(made, 9)
                pe.wait_ge(dve, 7)
                for b in range(KROW):
                    if b >= 2:
                        pe.wait_ge(evac, b - 1)
                    for j, row in enumerate((srcf_row, dstf_row, last_row)):
                        t = pe.transpose(bank[b % 2][:, j * P:(j + 1) * P], row[:, b, :], k.ident[:, :])
                    t.then_inc(turned, 1)
                pe.wait_ge(evac, KROW)
                pe.wait_ge(dve, 8)
                pe.matmul(bank[2][:, 0:NG], ends[:, :], k.dst_f[:, G - 1:NT:G], start=True, stop=True).then_inc(mm, 1)
                pe.wait_ge(dve, 12)
                pe.matmul(bank[3][:, 0:NS], ones[:, :], passed[:, :], start=True, stop=True).then_inc(mm, 1)


def project(nc, k, x, wts, biases):
    with ExitStack() as ctx:
        sb = lambda n, s, d: ctx.enter_context(nc.sbuf_tensor(n, s, d))
        x_sb = k.acc[:, :, 0:D]
        stats = sb("stats", [P, NW, 6], F32)
        mean_var = sb("mean_var", [P, NW, 2], F32)
        rstd = sb("rstd", [P, NW], F32)
        eps = sb("eps", [P, 1], F32)
        w_sb = sb("w_sb", [P, 2, 4 * D], F32)
        b_sb = sb("b_sb", [P, 4 * D], F32)
        xs = [sb(f"xs{i}", [P, 2 * D], F32) for i in range(2)]
        xt = [sb(f"xt{i}", [P, 2, P], F32) for i in range(2)]
        kv = [sb(f"kv{i}", [P, 2 * D], F32) for i in range(2)]
        qf = sb("qf", [P, D], F32)
        resid = sb("resid", [P, D], F32)
        xt_ps = ctx.enter_context(nc.psum_tensor("xt_ps", [P, 2, P], F32))
        kv_ps = [ctx.enter_context(nc.psum_tensor(f"kv_ps{i}", [P, 512], F32)) for i in range(2)]
        qs_ps = [ctx.enter_context(nc.psum_tensor(f"qs_ps{i}", [P, 512], F32)) for i in range(2)]
        names = ("pr_landed", "pr_padded", "pr_stats", "pr_aggr", "pr_sqrt", "pr_rstd", "pr_xn", "pr_turned", "pr_xt",
                 "pr_products", "pr_q", "pr_hi", "pr_resid", "pr_mid", "pr_kv", "pr_skip", "pr_xstored")
        (landed, padded, s_stats, s_aggr, s_sqrt, s_rstd, xn_ok, turned, xt_ok, prod_ok, q_ok, hi_ok, resid_ok,
         mid_ok, kv_ok, skip_ok, xstored) = (nc.alloc_semaphore(n) for n in names)
        kv_stored = [nc.alloc_semaphore(f"pr_kv_stored{i}") for i in range(2)]
        xs_stored = [nc.alloc_semaphore(f"pr_xs_stored{i}") for i in range(2)]
        half = NW // 2

        def windows(eng, body):
            body(0, 0, True, False)
            body(0, 1, True, False)
            with eng.Fori(1, half) as j:
                body(j, 0, False, False)
                body(j, 1, False, False)
            body(half, 0, False, True)

        with nc.Block() as block:
            @block.sync
            def _(sp):
                sp.wait_ge(padded, 1)
                sp.dma_start(x_sb[:, 0:NW - 1, :], x[0:(NW - 1) * P, :].rearrange("(w p) f -> p w f", p=P)).then_inc(landed, 16)
                sp.dma_start(x_sb[0:TAIL, NW - 1, :], x[(NW - 1) * P:N, :]).then_inc(landed, 16)
                for i in range(4):
                    sp.dma_start(w_sb[:, :, i * D:(i + 1) * D], wts[i].rearrange("(c p) n -> p c n", p=P)).then_inc(landed, 16)
                    sp.dma_start(b_sb[:, i * D:(i + 1) * D], bc(biases[i].unsqueeze(0), [P, D])).then_inc(landed, 16)
                sp.wait_ge(landed, 160)
                sp.dma_start(k.xs_d[:, 2 * D:3 * D].rearrange("(w p) f -> p w f", p=P), x_sb[:, :, :]).then_inc(xstored, 16)

                def store(j, s, first, last):
                    i = j * 2 + s
                    sp.wait_ge(kv_ok, i + 1)
                    sp.dma_start(k.kv_d[bass.ds(i * P, P), :], kv[s][:, :]).then_inc(kv_stored[s], 16)
                    sp.wait_ge(skip_ok, i + 1)
                    sp.dma_start(k.xs_d[bass.ds(i * P, P), 0:2 * D], xs[s][:, :]).then_inc(xs_stored[s], 16)
                windows(sp, store)
                sp.wait_ge(xstored, 16)
                for s in range(2):
                    sp.wait_ge(kv_stored[s], 16 * (half + 1 - s))
                    sp.wait_ge(xs_stored[s], 16 * (half + 1 - s))

            @block.scalar
            def _(act):
                act.wait_ge(s_aggr, 1)
                act.activation(rstd[:, :], mean_var[:, :, 1], ACT.Sqrt, bias=eps[:, :]).then_inc(s_sqrt, 1)

                def copy(j, s, first, last):
                    i = j * 2 + s
                    act.wait_ge(turned, i + 1)
                    if not first:
                        act.wait_ge(prod_ok, i - 1)
                    act.copy(xt[s][:, :, :], xt_ps[:, :, :]).then_inc(xt_ok, 1)
                windows(act, copy)

            @block.tensor
            def _(pe):
                pe.wait_ge(landed, 160)

                def turn(i, s, first):
                    pe.wait_ge(xn_ok, i + 1)
                    if not first:
                        pe.wait_ge(xt_ok, i)
                    for c in range(2):
                        t = pe.transpose(xt_ps[:, c, :], xs[s][:, c * P:(c + 1) * P], k.ident[:, :])
                    t.then_inc(turned, 1)

                def products(j, s, first, last):
                    i = j * 2 + s
                    if not last:
                        turn(i + 1, 1 - s, False)
                    pe.wait_ge(xt_ok, i + 1)
                    if not first:
                        pe.wait_ge(skip_ok, i - 1)
                    for c in range(2):
                        pe.matmul(kv_ps[s][:, :], xt[s][:, c, :], w_sb[:, c, 0:2 * D], start=(c == 0), stop=(c == 1))
                    for c in range(2):
                        m = pe.matmul(qs_ps[s][:, :], xt[s][:, c, :], w_sb[:, c, 2 * D:4 * D], start=(c == 0), stop=(c == 1))
                    m.then_inc(prod_ok, 1)
                turn(0, 0, True)
                windows(pe, products)

            @block.vector
            def _(v):
                v.memset(x_sb[:, NW - 1, :], 0.0).then_inc(padded, 1)
                v.memset(eps[:, :], EPS)
                v.wait_ge(landed, 160)
                with v.Fori(0, NW) as i:
                    v.bn_stats(stats[:, bass.ds(i, 1), :], x_sb[:, bass.ds(i, 1), :]).then_inc(s_stats, 1)
                v.wait_ge(s_stats, NW)
                for i in range(NW):
                    a = v.bn_aggr(mean_var[:, i, :], stats[:, i, :])
                a.then_inc(s_aggr, 1)
                v.wait_ge(s_sqrt, 1)
                v.reciprocal(rstd[:, :], rstd[:, :]).then_inc(s_rstd, 1)
                v.wait_ge(s_rstd, 1)

                def normalise(i, s, first):
                    if not first:
                        v.wait_ge(xs_stored[s], ((i - s) // 2) * 16 if isinstance(i, int) else (i - s) * 8)
                    v.tensor_scalar(xs[s][:, 0:D], x_sb[:, bass.ds(i, 1), :].rearrange("p a f -> p (a f)"),
                                    mean_var[:, bass.ds(i, 1), 0:1].rearrange("p a f -> p (a f)"), rstd[:, bass.ds(i, 1)],
                                    ALU.subtract, ALU.mult).then_inc(xn_ok, 1)

                def evacuate(j, s, first, last):
                    i = j * 2 + s
                    if not last:
                        normalise(i + 1, 1 - s, first and s == 0)
                    v.wait_ge(prod_ok, i + 1)
                    if not first:
                        v.wait_ge(kv_stored[s], j * 16)
                    v.tensor_tensor(qf[:, :], qs_ps[s][:, 0:D], b_sb[:, 2 * D:3 * D], ALU.add).then_inc(q_ok, 1)
                    v.tensor_tensor(kv[s][:, :], kv_ps[s][:, :], b_sb[:, 0:2 * D], ALU.add).then_inc(kv_ok, 1)
                    v.wait_ge(q_ok, i + 1)
                    q3 = k.q3[:, bass.ds(i, 1), :].rearrange("p a f -> p (a f)")
                    v.tensor_scalar(q3[:, 0:D], qf[:, :], 1.0, None, ALU.mult).then_inc(hi_ok, 1)
                    v.tensor_tensor(xs[s][:, D:2 * D], qs_ps[s][:, D:2 * D], b_sb[:, 3 * D:4 * D], ALU.add).then_inc(skip_ok, 1)
                    v.wait_ge(hi_ok, i + 1)
                    v.tensor_tensor(resid[:, :], qf[:, :], q3[:, 0:D], ALU.subtract).then_inc(resid_ok, 1)
                    v.wait_ge(resid_ok, i + 1)
                    v.tensor_scalar(q3[:, D:2 * D], resid[:, :], 1.0, None, ALU.mult).then_inc(mid_ok, 1)
                    v.wait_ge(mid_ok, i + 1)
                    v.tensor_tensor(q3[:, 2 * D:3 * D], resid[:, :], q3[:, D:2 * D], ALU.subtract)
                normalise(0, 0, True)
                windows(v, evacuate)


class Step:

    def __init__(self, base, offset):
        self.base, self.offset = base, offset

    def __add__(self, n):
        return Step(self.base, self.offset + n)

    @property
    def v(self):
        return self.base * LOOP + self.offset

    @property
    def slot(self):
        return self.offset % LOOP

    @property
    def turn(self):
        return self.base + self.offset // LOOP


def attend(nc, k):
    with ExitStack() as ctx:
        sb = lambda n, s, d: ctx.enter_context(nc.sbuf_tensor(n, s, d))
        ps = lambda n, s, d: ctx.enter_context(nc.psum_tensor(n, s, d))
        sem = nc.alloc_semaphore
        KV = [sb(f"KV{i}", [P, G, 2 * D], F32) for i in range(LOOP)]
        idx = [sb(f"idx{i}", [P, G], I32) for i in range(LOOP)]
        oh = [sb(f"oh{i}", [P, G, P], BF16) for i in range(LOOP)]
        ohT = [sb(f"ohT{i}", [P, G, P], BF16) for i in range(LOOP)]
        oh32 = [sb(f"oh32_{i}", [P, G, P], F32) for i in range(2)]
        reset = [sb(f"reset{i}", [TG, P], F32) for i in range(LOOP)]
        rel = [sb(f"rel{i}", [P, G], F32) for i in range(LOOP)]
        prod = sb("prod", [P, G, D], F32)
        lg = [sb(f"lg{i}", [P, TG], F32) for i in range(2)]
        running = sb("running", [TG, P], F32)
        seg_max = sb("seg_max", [P, G, HEADS], BF16)
        tile_max = sb("tile_max", [P, HEADS], F32)
        m_new = sb("m_new", [P, HEADS], BF16)
        m_fall = sb("m_fall", [P, HEADS], F32)
        fac = [sb(f"fac{i}", [P, HEADS], F32) for i in range(2)]
        dl = sb("dl", [P, TG], F32)
        msg = sb("msg", [P, G, HEADS, HW], F32)
        Q = [ps(f"Q{i}", [P, G, D], F32) for i in range(2)]
        ohT_ps = ps("ohT_ps", [P, G, P], BF16)
        small_ps = ps("small_ps", [P, 4, P], F32)
        lgT_ps, runT_ps, ref_ps = small_ps[0:TG, 0, :], small_ps[:, 1, 0:TG], small_ps[:, 2, 0:TG]
        max_ps = ps("max_ps", [P, 512], F32)
        agg_ps = ps("agg_ps", [P, 512], F32)
        names = ("idx", "rel", "oh", "turned", "ohT", "q", "prod", "lg", "lgT", "running", "runT", "seg_max", "max",
                 "tile_max", "m_new", "m_fall", "m_all", "fac", "ref", "dl", "p", "msg", "oh32", "agg", "scaled", "acc", "cleared", "idx_seen")
        ok = {n: sem(f"at_{n}") for n in names}
        kv_landed = [sem(f"at_kv_landed{i}") for i in range(LOOP)]
        reset_landed = [sem(f"at_reset_landed{i}") for i in range(LOOP)]

        def walk(eng, body):
            body(Step(0, 0), True)
            with eng.Fori(0, (RUN - 1) // LOOP) as j:
                for c in range(LOOP):
                    body(Step(j, c + 1), False)

        def load(eng, tab, s, hi):
            i = s.v
            return eng.value_load(tab[0:1, bass.ds(i, 1)], min_val=0, max_val=hi)

        with nc.Block() as block:
            @block.gpsimd
            def _(pool):
                def gather(s, first):
                    if not first:
                        pool.wait_ge(ok["msg"], s.v - (LOOP - 1))
                    g = load(pool, k.g_tab, s, NT - G)
                    pool.tensor_copy(idx[s.slot][:, :], k.src_i[:, bass.ds(g, G)]).then_inc(ok["idx"], 1)
                    pool.wait_ge(ok["idx"], s.v + 1)
                    pool.sem_inc(ok["idx_seen"], 1)
                    for t in range(G):
                        pool.indirect_dma_start(out=KV[s.slot][:, t, :], out_offset=None, in_=k.kv_d,
                                                in_offset=bass.IndirectOffsetOnAxis(ap=idx[s.slot][:, t:t + 1], axis=0)
                                                ).then_inc(kv_landed[s.slot], 16)
                for i in range(LOOP):
                    gather(Step(0, i), True)
                with pool.Fori(1, NS // LOOP) as j:
                    for c in range(LOOP):
                        gather(Step(j, c), False)
                for s in kv_landed:
                    pool.wait_ge(s, 16 * G * (NS // LOOP))

            @block.sync
            def _(sp):
                def resets(s, first):
                    if not first:
                        sp.wait_ge(ok["running"], s.v - (LOOP - 1))
                    g = load(sp, k.g_tab, s, NT - G)
                    sp.dma_start(reset[s.slot][:, :], k.reset_d[bass.ds(g, G), :, :].rearrange("t h p -> (t h) p")
                                 ).then_inc(reset_landed[s.slot], 16)
                for i in range(LOOP):
                    resets(Step(0, i), True)
                with sp.Fori(1, NS // LOOP) as j:
                    for c in range(LOOP):
                        resets(Step(j, c), False)
                for s in reset_landed:
                    sp.wait_ge(s, 16 * (NS // LOOP))

            @block.vector
            def _(v):
                def one_hot(s):
                    g = load(v, k.g_tab, s, NT - G)
                    v.tensor_scalar(rel[s.slot][:, :], k.dst_f[:, bass.ds(g, G)], k.wbase[:, bass.ds(s.v, 1)], None,
                                    ALU.subtract).then_inc(ok["rel"], 1)
                    v.wait_ge(ok["rel"], s.v + 1)
                    for t in range(G):
                        o = v.tensor_scalar(oh[s.slot][:, t, :], k.iota_b[:, :], rel[s.slot][:, t:t + 1], None, ALU.is_equal)
                    o.then_inc(ok["oh"], 1)

                def product(s):
                    v.wait_ge(kv_landed[s.slot], (s.turn + 1) * (16 * G))
                    v.wait_ge(ok["q"], s.v + 1)
                    v.tensor_tensor(prod[:, :, :], KV[s.slot][:, :, 0:D], Q[s.offset % 2][:, :, :], ALU.mult).then_inc(ok["prod"], 1)

                def logits(s):
                    v.wait_ge(ok["prod"], s.v + 1)
                    v.reduce_sum(lg[s.offset % 2][:, :], prod[:, :, :].rearrange("p t (h d) -> p (t h) d", d=DH), AX.X
                                 ).then_inc(ok["lg"], 1)

                def accumulate(s):
                    w = load(v, k.w_tab, s, NW - 1)
                    acc = k.acc[:, bass.ds(w, 1), :].rearrange("p a (h e) -> p (a h) e", e=HW)
                    v.wait_ge(ok["fac"], s.v + 1)
                    v.wait_ge(ok["acc"], s.v + 1)
                    v.tensor_tensor(acc, acc, bc(fac[s.offset % 2][:, :].unsqueeze(2), [P, HEADS, HW]), ALU.mult).then_inc(ok["scaled"], 1)
                    v.wait_ge(ok["agg"], s.v + 1)
                    v.wait_ge(ok["scaled"], s.v + 1)
                    v.tensor_tensor(acc, acc, agg_ps[:, 0:HEADS * HW].rearrange("p (h e) -> p h e", e=HW), ALU.add).then_inc(ok["acc"], 1)

                def body(s, first):
                    v.wait_ge(ok["lgT"], s.v + 1)
                    v.wait_ge(reset_landed[s.slot], (s.turn + 1) * 16)
                    v.tensor_tensor_scan(running[:, :], reset[s.slot][:, :], lgT_ps, -BIG, ALU.add, ALU.max).then_inc(ok["running"], 1)
                    product(s + 1)
                    g = load(v, k.g_tab, s, NT - G)
                    v.wait_ge(ok["runT"], s.v + 1)
                    v.scalar_tensor_tensor(out=seg_max[:, :, :], in0=bc(k.last_b[:, bass.ds(g, G)].unsqueeze(2), [P, G, HEADS]),
                                           scalar=1.0 / BIG, in1=runT_ps.rearrange("p (t h) -> p t h", h=HEADS),
                                           op0=ALU.mult, op1=ALU.mult).then_inc(ok["seg_max"], 1)
                    one_hot(s + 2)
                    w = load(v, k.w_tab, s, NW - 1)
                    m_all = k.m_all[:, bass.ds(w, 1), :].rearrange("p a h -> p (a h)")
                    v.wait_ge(ok["max"], s.v + 1)
                    v.tensor_reduce(tile_max[:, :], max_ps[:, 0:TG].rearrange("p (t h) -> p h t", h=HEADS), AX.X, ALU.max).then_inc(ok["tile_max"], 1)
                    v.wait_ge(ok["tile_max"], s.v + 1)
                    if not first:
                        v.wait_ge(ok["m_all"], s.v)
                    v.tensor_tensor(m_new[:, :], m_all, tile_max[:, :], ALU.max).then_inc(ok["m_new"], 1)
                    v.wait_ge(ok["m_new"], s.v + 1)
                    v.tensor_tensor(m_fall[:, :], m_all, m_new[:, :], ALU.subtract).then_inc(ok["m_fall"], 1)
                    logits(s + 1)
                    v.wait_ge(ok["m_fall"], s.v + 1)
                    v.tensor_scalar(m_all, m_new[:, :], 1.0, None, ALU.mult).then_inc(ok["m_all"], 1)
                    v.wait_ge(ok["ref"], s.v + 1)
                    v.tensor_tensor(dl[:, :], lg[s.offset % 2][:, :], ref_ps, ALU.subtract).then_inc(ok["dl"], 1)
                    if not first:
                        accumulate(s + (-1))
                    v.wait_ge(ok["p"], s.v + 1)
                    v.tensor_tensor(msg[:, :, :, 0:DH], KV[s.slot][:, :, D:2 * D].rearrange("p t (h d) -> p t h d", d=DH),
                                    bc(msg[:, :, :, DH:HW], [P, G, HEADS, DH]), ALU.mult).then_inc(ok["msg"], 1)

                v.memset(k.acc[:, :, :], 0.0).then_inc(ok["acc"], 1)
                v.memset(k.m_all[:, :, :], -BIG).then_inc(ok["cleared"], 1)
                one_hot(Step(0, 0))
                one_hot(Step(0, 1))
                product(Step(0, 0))
                logits(Step(0, 0))
                v.wait_ge(ok["cleared"], 1)
                walk(v, body)
                accumulate(Step((RUN - 1) // LOOP, 0))

            @block.scalar
            def _(act):
                def turn_copy(s):
                    act.wait_ge(ok["turned"], s.v + 1)
                    act.copy(ohT[s.slot][:, :, :], ohT_ps[:, :, :]).then_inc(ok["ohT"], 1)

                def body(s, first):
                    act.wait_ge(ok["oh"], s.v + 1)
                    act.copy(oh32[s.offset % 2][:, :, :], oh[s.slot][:, :, :]).then_inc(ok["oh32"], 1)
                    turn_copy(s + 2)
                    act.wait_ge(ok["m_fall"], s.v + 1)
                    act.activation(fac[s.offset % 2][:, :], m_fall[:, :], ACT.Exp, scale=SCALE).then_inc(ok["fac"], 1)
                    act.wait_ge(ok["dl"], s.v + 1)
                    if not first:
                        act.wait_ge(ok["agg"], s.v)
                    act.activation(msg[:, :, :, DH:HW], dl[:, :].rearrange("p (t h a) -> p t h a", h=HEADS, a=1), ACT.Exp,
                                   scale=SCALE).then_inc(ok["p"], 1)
                turn_copy(Step(0, 0))
                turn_copy(Step(0, 1))
                walk(act, body)

            @block.tensor
            def _(pe):
                def turn(s):
                    pe.wait_ge(ok["oh"], s.v + 1)
                    for t in range(G):
                        m = pe.transpose(ohT_ps[:, t, :], oh[s.slot][:, t, :], k.ident_b[:, :])
                    m.then_inc(ok["turned"], 1)

                def queries(s):
                    w = load(pe, k.w_tab, s, NW - 1)
                    pe.wait_ge(ok["ohT"], s.v + 1)
                    for t in range(G):
                        for c in range(3):
                            m = pe.matmul(Q[s.offset % 2][:, t, :], ohT[s.slot][:, t, :],
                                          k.q3[:, bass.ds(w, 1), c * D:(c + 1) * D].rearrange("p a f -> p (a f)"),
                                          start=(c == 0), stop=(c == 2))
                    m.then_inc(ok["q"], 1)

                def turn_logits(s):
                    pe.wait_ge(ok["lg"], s.v + 1)
                    pe.transpose(lgT_ps, lg[s.offset % 2][:, :], k.ident[:, :]).then_inc(ok["lgT"], 1)

                def body(s, first):
                    pe.wait_ge(ok["running"], s.v + 1)
                    g = load(pe, k.g_tab, s, NT - G)
                    pe.transpose(runT_ps, running[:, :], k.ident[0:TG, 0:TG]).then_inc(ok["runT"], 1)
                    pe.wait_ge(ok["seg_max"], s.v + 1)
                    for t in range(G):
                        at = max_ps[:, t * HEADS:(t + 1) * HEADS]
                        pe.matmul(at, k.ones_b[:, :], k.negbig[:, 0:HEADS], start=True, stop=False)
                        pe.matmul(at, oh[s.slot][:, t, :], bc(k.last_b[:, bass.ds(g + t, 1)], [P, HEADS]), start=False, stop=False)
                        m = pe.matmul(at, oh[s.slot][:, t, :], seg_max[:, t, :], start=False, stop=True)
                    m.then_inc(ok["max"], 1)
                    turn(s + 2)
                    pe.wait_ge(ok["m_new"], s.v + 1)
                    for t in range(G):
                        m = pe.matmul(ref_ps[:, t * HEADS:(t + 1) * HEADS], ohT[s.slot][:, t, :], m_new[:, :], start=True, stop=True)
                    m.then_inc(ok["ref"], 1)
                    queries(s + 2)
                    pe.wait_ge(ok["dl"], s.v + 1)
                    turn_logits(s + 1)
                    pe.wait_ge(ok["oh32"], s.v + 1)
                    pe.wait_ge(ok["msg"], s.v + 1)
                    for t in range(G):
                        m = pe.matmul(agg_ps[:, 0:HEADS * HW], oh32[s.offset % 2][:, t, :],
                                      msg[:, t, :, :].rearrange("p h e -> p (h e)"), start=(t == 0), stop=(t == G - 1))
                    m.then_inc(ok["agg"], 1)
                for i in range(2):
                    turn(Step(0, i))
                    queries(Step(0, i))
                turn_logits(Step(0, 0))
                walk(pe, body)


def pairs(eng, half, body):
    body(0, 0, True, False)
    body(0, 1, True, False)
    with eng.Fori(1, half) as j:
        body(j, 0, False, False)
        body(j, 1, False, False)
    body(half, 0, False, True)


class Chain:

    def __init__(self, eng, sem, turn, per_turn):
        self.eng, self.sem, self.base, self.n, self.per_turn = eng, sem, turn * per_turn, 0, per_turn

    def on(self, ins):
        self.n += 1
        assert self.n <= self.per_turn
        ins.then_inc(self.sem, 1)

    def wait(self):
        self.eng.wait_ge(self.sem, self.base + self.n)

    def done(self):
        assert self.n == self.per_turn, self.n


def node_update(nc, k, gamma, beta, w_gat):
    with ExitStack() as ctx:
        sb = lambda n, s, d: ctx.enter_context(nc.sbuf_tensor(n, s, d))
        ps = lambda n, s, d: ctx.enter_context(nc.psum_tensor(n, s, d))
        xs = [sb(f"nu_xs{i}", [P, CW, 3 * D], F32) for i in range(2)]
        den = sb("nu_den", [P, CW, HEADS, 1], F32)
        out = sb("nu_out", [P, CW, D], F32)
        x2 = [sb(f"nu_x2_{i}", [P, CW, D], F32) for i in range(2)]
        xn2 = sb("nu_xn2", [P, CW, D], F32)
        gam = sb("nu_gam", [P, D], F32)
        bet = sb("nu_bet", [P, D], F32)
        wg = sb("nu_wg", [P, 2, RD], F32)
        stats = sb("nu_stats", [P, CW, 6], F32)
        mv = sb("nu_mv", [P, CW, 2], F32)
        rstd = sb("nu_rstd", [P, CW], F32)
        eps = sb("nu_eps", [P, 1], F32)
        turn_ps = [ps(f"nu_turn{i}", [P, 4, P], F32) for i in range(4)]
        h_ps = [ps(f"nu_h{i}", [RD, 512], F32) for i in range(2)]
        const, ready, dve, s_stats, s_in, s_gelu, s_var, s_sqrt, turned, xt_ok, h_ok, h_read = (
            nc.alloc_semaphore(f"nu_{n}") for n in ("constants", "eps", "dve", "stats", "preact", "gelu", "variance", "sqrt", "turned", "xT", "h", "h_read"))
        landed = [nc.alloc_semaphore(f"nu_landed{i}") for i in range(2)]
        stored = [nc.alloc_semaphore(f"nu_stored{i}") for i in range(2)]
        half, K = NB // 2, 43
        HALFN = CN // 2
        parts = ((0, 4), (4, CW))
        with nc.Block() as block:
            @block.sync
            def _(sp):
                sp.dma_start(gam[:, :], bc(gamma.unsqueeze(0), [P, D])).then_inc(const, 16)
                sp.dma_start(bet[:, :], bc(beta.unsqueeze(0), [P, D])).then_inc(const, 16)
                sp.dma_start(wg[:, :, :], w_gat.rearrange("(c p) n -> p c n", p=P)).then_inc(const, 16)

                def load(i, s):
                    sp.dma_start(xs[s][:, :, :], k.xs_d[bass.ds(i * CN, CN), :].rearrange("(w p) f -> p w f", p=P)).then_inc(landed[s], 16)

                def turn(j, s, first, last):
                    i = j * 2 + s
                    sp.wait_ge(dve, (i + 1) * K)
                    sp.dma_start(k.x2_d[bass.ds(i * CN, CN), :].rearrange("(w p) f -> p w f", p=P), x2[s][:, :, :]).then_inc(stored[s], 16)
                    if not last:
                        load(i + 2, s)
                load(0, 0)
                load(1, 1)
                for i in range(2):
                    turn(0, i, True, False)
                with sp.Fori(1, half - 1) as j:
                    turn(j, 0, False, False)
                    turn(j, 1, False, False)
                turn(half - 1, 0, False, False)
                turn(half - 1, 1, False, True)
                turn(half, 0, False, True)
                for s in range(2):
                    sp.wait_ge(stored[s], 16 * (half + 1 - s))

            @block.vector
            def _(v):
                v.memset(eps[:, :], EPS).then_inc(ready, 1)
                v.wait_ge(const, 48)

                def normalise(ch, src, dst, nth):
                    for w in range(CW):
                        ch.on(v.bn_stats(stats[:, w, :], src[:, w, :]))
                    ch.wait()
                    v.sem_inc(s_stats, 1)
                    for w in range(CW):
                        a = v.bn_aggr(mv[:, w, :], stats[:, w, :])
                    a.then_inc(s_var, 1)
                    v.wait_ge(s_sqrt, nth)
                    ch.on(v.reciprocal(rstd[:, :], rstd[:, :]))
                    ch.wait()
                    for w in range(CW):
                        ch.on(v.tensor_scalar(dst[:, w, :], src[:, w, :], mv[:, w, 0:1], rstd[:, w:w + 1], ALU.subtract, ALU.mult))
                    ch.wait()

                def turn(j, s, first, last):
                    i = j * 2 + s
                    ch = Chain(v, dve, i, K)
                    acc = k.acc[:, bass.ds(i * CW, CW), :].rearrange("p w (h e) -> p w h e", e=HW)
                    v4 = lambda t: t.rearrange("p w (h d) -> p w h d", d=DH)
                    ch.on(v.tensor_scalar(den[:, :, :, :], acc[:, :, :, DH:HW], 1e-30, None, ALU.max))
                    ch.wait()
                    ch.on(v.reciprocal(den[:, :, :, :], den[:, :, :, :]))
                    ch.wait()
                    for w in range(CW):
                        ch.on(v.tensor_tensor(v4(out[:, :, :])[:, w], k.acc[:, bass.ds(i * CW + w, 1), :].rearrange("p a (h e) -> p (a h) e", e=HW)[:, :, 0:DH],
                                              bc(den[:, w, :, :], [P, HEADS, DH]), ALU.mult))
                    ch.wait()
                    v.wait_ge(landed[s], j * 16 + 16)
                    v.tensor_tensor(out[:, :, :], out[:, :, :], xs[s][:, :, D:2 * D], ALU.add).then_inc(s_in, 1)
                    v.wait_ge(s_gelu, i + 1)
                    ch.on(v.tensor_tensor(out[:, :, :], out[:, :, :], xs[s][:, :, 0:D], ALU.add))
                    ch.wait()
                    if not first:
                        v.wait_ge(stored[s], j * 16)
                    normalise(ch, out, x2[s], i * 2 + 1)
                    ch.on(v.tensor_tensor(x2[s][:, :, :], x2[s][:, :, :], bc(gam[:, :].unsqueeze(1), [P, CW, D]), ALU.mult))
                    ch.wait()
                    ch.on(v.tensor_tensor(x2[s][:, :, :], x2[s][:, :, :], bc(bet[:, :].unsqueeze(1), [P, CW, D]), ALU.add))
                    ch.wait()
                    ch.on(v.tensor_tensor(x2[s][:, :, :], x2[s][:, :, :], xs[s][:, :, 2 * D:3 * D], ALU.add))
                    ch.wait()
                    if not (isinstance(i, int) and i == 0):
                        v.wait_ge(turned, i)
                    normalise(ch, x2[s], xn2, i * 2 + 2)
                    ch.done()
                    v.wait_ge(h_ok, i + 1)
                    for q in range(2):
                        r = v.tensor_copy(k.hT[:, bass.ds(i * CN + q * HALFN, HALFN)], h_ps[q][:, 0:HALFN])
                    r.then_inc(h_read, 1)
                pairs(v, half, turn)

            @block.scalar
            def _(act):
                act.wait_ge(ready, 1)

                def root(n):
                    act.wait_ge(s_var, n)
                    act.activation(rstd[:, :], mv[:, :, 1], ACT.Sqrt, bias=eps[:, :]).then_inc(s_sqrt, 1)

                def turn(j, s, first, last):
                    i = j * 2 + s
                    act.wait_ge(s_in, i + 1)
                    act.activation(out[:, :, :], out[:, :, :], ACT.Gelu).then_inc(s_gelu, 1)
                    root(i * 2 + 1)
                    root(i * 2 + 2)
                    act.wait_ge(turned, i + 1)
                    for c in range(2):
                        for q, (a, b) in enumerate(parts):
                            r = act.copy(k.xT[:, c, bass.ds(i * CN + a * P, (b - a) * P)],
                                         turn_ps[2 * c + q][:, 0:b - a, :].rearrange("p w n -> p (w n)"))
                    r.then_inc(xt_ok, 1)
                pairs(act, half, turn)

            @block.tensor
            def _(pe):
                pe.wait_ge(const, 48)

                def turn(j, s, first, last):
                    i = j * 2 + s
                    pe.wait_ge(dve, (i + 1) * K)
                    for c in range(2):
                        for q, (a, b) in enumerate(parts):
                            for w in range(a, b):
                                t = pe.transpose(turn_ps[2 * c + q][:, w - a, :], xn2[:, w, c * P:(c + 1) * P], k.ident[:, :])
                    t.then_inc(turned, 1)
                    pe.wait_ge(xt_ok, i + 1)
                    if not (isinstance(i, int) and i == 0):
                        pe.wait_ge(h_read, i)
                    for q in range(2):
                        for c in range(2):
                            m = pe.matmul(h_ps[q][:, 0:HALFN], wg[:, c, :], k.xT[:, c, bass.ds(i * CN + q * HALFN, HALFN)],
                                          start=(c == 0), stop=(c == 1))
                    m.then_inc(h_ok, 1)
                pairs(pe, half, turn)


def route_tables(nc, k, edge_index, att_src, att_dst):
    with ExitStack() as ctx:
        sb = lambda n, s, d: ctx.enter_context(nc.sbuf_tensor(n, s, d))
        ends = sb("rt_ends", [P, 2, RT], I32)
        dstf = sb("rt_dstf", [P, RT], F32)
        a_idx = sb("rt_a", [P, RT], F32)
        ge = sb("rt_ge", [P, RT], F32)
        iota6 = sb("rt_iota6", [P, BLK], F32)
        att = sb("rt_att", [P, 2, RD], F32)
        tmp = sb("rt_tmp", [P, NW, RD], F32)
        part = sb("rt_part", [P, 1], F32)
        valid = sb("rt_valid", [P, 2], F32)
        masked = sb("rt_masked", [P, NW, RH], F32)
        top = sb("rt_top", [P, 2, RH], F32)
        hn_ps = [ctx.enter_context(nc.psum_tensor(f"rt_h{i}", [P, 32, RD], F32)) for i in range(2)]
        landed, made, dve, turned, top_in, top_ok, tab, stored = (nc.alloc_semaphore(f"rt_{n}") for n in (
            "landed", "constants", "dve", "turned", "max_in", "max", "tables", "stored"))
        with nc.Block() as block:
            @block.sync
            def _(sp):
                sp.dma_start(ends[:, :, :], edge_index.rearrange("a (p c) -> p a c", p=P)).then_inc(landed, 16)
                for i, a in enumerate((att_src, att_dst)):
                    sp.dma_start(att[:, i, :], bc(a.rearrange("h e -> (h e)").unsqueeze(0), [P, RD])).then_inc(landed, 16)
                sp.wait_ge(tab, 1)
                sp.dma_start(k.src_tab_d.rearrange("(w p) f -> p w f", p=P), k.node_src[:, :, :]).then_inc(stored, 16)
                sp.dma_start(k.dst_tab_d.rearrange("(w p) f -> p w f", p=P), k.node_dst[:, :, :]).then_inc(stored, 16)
                sp.wait_ge(stored, 32)

            @block.gpsimd
            def _(pool):
                pool.iota(iota6[:, :], [[1, BLK]], base=0, channel_multiplier=0, allow_small_or_imprecise_dtypes=True).then_inc(made, 1)
                pool.iota(part[:, :], [[0, 1]], base=0, channel_multiplier=1, allow_small_or_imprecise_dtypes=True).then_inc(made, 1)
                pool.iota(k.iota_span[:, :], [[1, 3 * CH]], base=0, channel_multiplier=0, allow_small_or_imprecise_dtypes=True).then_inc(made, 1)
                pool.wait_ge(top_in, 1)
                pool.partition_all_reduce(top[:, 1, :], top[:, 0, :], P, bass.bass_isa.ReduceOp.max).then_inc(top_ok, 1)

            @block.tensor
            def _(pe):
                for w in range(NW):
                    t = pe.transpose(hn_ps[w // 32][:, w % 32, :], k.hT[:, w * P:(w + 1) * P], k.ident[0:RD, 0:RD])
                t.then_inc(turned, 1)

            @block.vector
            def _(v):
                d = Count(dve)
                on = d.on
                wait = lambda: v.wait_ge(dve, d.n)
                v.wait_ge(turned, 1)
                on(v.tensor_copy(k.node_src[:, 0:32, 0:RD], hn_ps[0][:, :, :]))
                on(v.tensor_copy(k.node_src[:, 32:NW, 0:RD], hn_ps[1][:, 0:NW - 32, :]))
                v.wait_ge(landed, 48)
                v.wait_ge(made, 3)
                wait()
                a_src, a_dst = k.node_src[:, :, RD:RV], k.node_dst[:, :, 0:RH]
                for i, a in enumerate((a_src, a_dst)):
                    on(v.tensor_tensor(tmp[:, :, :], k.node_src[:, :, 0:RD], bc(att[:, i:i + 1, :], [P, NW, RD]), ALU.mult))
                    wait()
                    on(v.reduce_sum(a, tmp[:, :, :].rearrange("p w (h e) -> p w h e", e=NE), AX.X))
                    wait()
                on(v.tensor_scalar(valid[:, 0:1], part[:, :], float(TAIL), None, ALU.is_lt))
                wait()
                on(v.tensor_scalar(valid[:, 1:2], valid[:, 0:1], BIG, -BIG, ALU.mult, ALU.add))
                on(v.tensor_copy(masked[:, 0:NW - 1, :], k.node_src[:, 0:NW - 1, RD:RV]))
                wait()
                on(v.tensor_scalar(masked[:, NW - 1, :], k.node_src[:, NW - 1, RD:RV], valid[:, 0:1], valid[:, 1:2], ALU.mult, ALU.add))
                wait()
                v.tensor_reduce(top[:, 0, :], masked[:, :, :].rearrange("p w h -> p h w"), AX.X, ALU.max).then_inc(top_in, 1)
                v.wait_ge(top_ok, 1)
                on(v.tensor_tensor(masked[:, :, :], a_dst, bc(top[:, 1:2, :], [P, NW, RH]), ALU.add))
                wait()
                v.scalar_tensor_tensor(out=k.node_dst[:, :, RH:2 * RH], in0=masked[:, :, :], scalar=0.2, in1=masked[:, :, :],
                                       op0=ALU.mult, op1=ALU.max).then_inc(tab, 1)
                for i in range(2):
                    on(v.tensor_scalar(k.ends[:, :, i, :], ends[:, i, :].rearrange("p (s t) -> p s t", t=RG), float(N - 1), None, ALU.min))
                on(v.tensor_copy(dstf[:, :], ends[:, 1, :]))
                wait()
                on(v.tensor_scalar(a_idx[:, :], dstf[:, :], float(SPAN), None, ALU.is_ge))
                wait()
                for a in range(2, BLK):
                    on(v.tensor_scalar(ge[:, :], dstf[:, :], float(SPAN * a), None, ALU.is_ge))
                    wait()
                    on(v.tensor_tensor(a_idx[:, :], a_idx[:, :], ge[:, :], ALU.add))
                    wait()
                on(v.scalar_tensor_tensor(out=k.column[:, :], in0=a_idx[:, :], scalar=-float(SPAN), in1=dstf[:, :], op0=ALU.mult, op1=ALU.add))
                on(v.tensor_tensor(k.block_oh[:, :, :], bc(a_idx[:, :].unsqueeze(2), [P, RT, BLK]), bc(iota6[:, :].unsqueeze(1), [P, RT, BLK]), ALU.is_equal))
                wait()


def route_edges(nc, k):
    with ExitStack() as ctx:
        sb = lambda n, s, d: ctx.enter_context(nc.sbuf_tensor(n, s, d))
        idx = [sb(f"re_idx{i}", [P, 2 * RG], I32) for i in range(2)]
        gs = [sb(f"re_src{i}", [P, RG, RV], F32) for i in range(2)]
        gd = [sb(f"re_dst{i}", [P, RG, 2 * RH], F32) for i in range(2)]
        e = [sb(f"re_e{i}", [P, RG, RH], F32) for i in range(3)]
        val = sb("re_val", [P, RG, RV], F32)
        rest = sb("re_rest", [P, RG, RV], F32)
        split = [sb(f"re_split{i}", [P, RG, RV], BF16) for i in range(3)]
        spread = [[sb(f"re_spread{i}_{c}", [P, RG, BLK * RV], BF16) for c in range(3)] for i in range(2)]
        col_oh = [sb(f"re_col{t}", [P, 3 * CH], BF16) for t in range(RG)]
        zero = sb("re_zero", [P, 3 * CH], BF16)
        acc = [ctx.enter_context(nc.psum_tensor(f"re_acc{i}", [P, 512], F32)) for i in range(3)]
        names = ("idx", "idx_seen", "dve", "ee", "spread", "column", "tile", "zero", "last")
        ok = {n: nc.alloc_semaphore(f"re_{n}") for n in names}
        landed = [nc.alloc_semaphore(f"re_landed{i}") for i in range(2)]
        K = 8

        def walk(eng, body):
            body(0, 0, True)
            body(0, 1, True)
            with eng.Fori(1, RSTEPS // 2) as j:
                body(j, 0, False)
                body(j, 1, False)

        with nc.Block() as block:
            @block.gpsimd
            def _(pool):

                def gather(j, s, first):
                    i = j * 2 + s
                    if not first:
                        pool.wait_ge(ok["dve"], (i - 2) * K + 4)
                    pool.tensor_copy(idx[s][:, :], k.ends[:, bass.ds(i, 1), :, :].rearrange("p a b t -> p (a b t)")).then_inc(ok["idx"], 1)
                    pool.wait_ge(ok["idx"], i + 1)
                    pool.sem_inc(ok["idx_seen"], 1)
                    for t in range(RG):
                        pool.indirect_dma_start(out=gs[s][:, t, :], out_offset=None, in_=k.src_tab_d,
                                                in_offset=bass.IndirectOffsetOnAxis(ap=idx[s][:, t:t + 1], axis=0)).then_inc(landed[s], 16)
                        pool.indirect_dma_start(out=gd[s][:, t, :], out_offset=None, in_=k.dst_tab_d,
                                                in_offset=bass.IndirectOffsetOnAxis(ap=idx[s][:, RG + t:RG + t + 1], axis=0)).then_inc(landed[s], 16)
                walk(pool, gather)

            @block.scalar
            def _(act):
                def body(j, s, first):
                    i = j * 2 + s
                    act.wait_ge(ok["dve"], i * K + 3)
                    act.activation(val[:, :, RD:RV], e[2][:, :, :], ACT.Exp).then_inc(ok["ee"], 1)
                walk(act, body)

            @block.vector
            def _(v):
                v.memset(zero[:, :], 0.0).then_inc(ok["zero"], 1)

                def body(j, s, first):
                    i = j * 2 + s
                    ch = Chain(v, ok["dve"], i, K)
                    v.wait_ge(landed[s], (j + 1) * (32 * RG))
                    ch.on(v.tensor_tensor(e[0][:, :, :], gs[s][:, :, RD:RV], gd[s][:, :, 0:RH], ALU.add))
                    ch.wait()
                    ch.on(v.scalar_tensor_tensor(out=e[1][:, :, :], in0=e[0][:, :, :], scalar=0.2, in1=e[0][:, :, :], op0=ALU.mult, op1=ALU.max))
                    ch.wait()
                    ch.on(v.tensor_tensor(e[2][:, :, :], e[1][:, :, :], gd[s][:, :, RH:2 * RH], ALU.subtract))
                    ch.wait()
                    v.wait_ge(ok["ee"], i + 1)
                    for t in range(RG):
                        m = v.tensor_tensor(val[:, t, 0:RD].rearrange("p (h e) -> p h e", e=NE), gs[s][:, t, 0:RD].rearrange("p (h e) -> p h e", e=NE),
                                            bc(val[:, t, RD:RV].unsqueeze(2), [P, RH, NE]), ALU.mult)
                    ch.on(m)
                    ch.wait()
                    if not (first and s == 0):
                        v.wait_ge(ok["spread"], i)
                    ch.on(v.tensor_copy(split[0][:, :, :], val[:, :, :]))
                    ch.wait()
                    ch.on(v.tensor_tensor(rest[:, :, :], val[:, :, :], split[0][:, :, :], ALU.subtract))
                    ch.wait()
                    ch.on(v.tensor_copy(split[1][:, :, :], rest[:, :, :]))
                    ch.wait()
                    ch.on(v.tensor_tensor(split[2][:, :, :], rest[:, :, :], split[1][:, :, :], ALU.subtract))
                    ch.wait()
                    if not first:
                        v.wait_ge(ok["tile"], (i - 1) * RG)
                    for c in range(3):
                        for t in range(RG):
                            m = v.tensor_tensor(spread[s][c][:, t, :].rearrange("p (a v) -> p a v", a=BLK),
                                                bc(k.block_oh[:, bass.ds(i * RG + t, 1), :].rearrange("p a b -> p (a b)").unsqueeze(2), [P, BLK, RV]),
                                                bc(split[c][:, t:t + 1, :], [P, BLK, RV]), ALU.mult)
                    m.then_inc(ok["spread"], 1)
                    for t in range(RG):
                        if not (first and s == 0):
                            v.wait_ge(ok["tile"], (i - 1) * RG + t + 1)
                        v.tensor_scalar(col_oh[t][:, :], k.iota_span[:, :], k.column[:, bass.ds(i * RG + t, 1)], None, ALU.is_equal).then_inc(ok["column"], 1)
                walk(v, body)
                v.wait_ge(ok["last"], 1)
                for c in range(3):
                    r = v.tensor_copy(k.sums[:, c * CH:(c + 1) * CH], acc[c][0:BLK * RV, 0:CH])
                r.then_inc(ok["last"], 1)

            @block.tensor
            def _(pe):
                pe.wait_ge(ok["zero"], 1)
                for c in range(3):
                    pe.matmul(acc[c][0:BLK * RV, 0:CH], zero[:, 0:BLK * RV], zero[:, 0:CH], start=True, stop=False)

                def body(j, s, first):
                    i = j * 2 + s
                    pe.wait_ge(ok["spread"], i + 1)
                    for t in range(RG):
                        pe.wait_ge(ok["column"], i * RG + t + 1)
                        for q in range(3):
                            for c in range(3):
                                m = pe.matmul(acc[c][0:BLK * RV, 0:CH], spread[s][q][:, t, :], col_oh[t][:, c * CH:(c + 1) * CH],
                                              start=False, stop=False)
                        m.then_inc(ok["tile"], 1)
                walk(pe, body)
                for c in range(3):
                    m = pe.matmul(acc[c][0:BLK * RV, 0:CH], zero[:, 0:BLK * RV], zero[:, 0:CH], start=False, stop=True)
                m.then_inc(ok["last"], 1)


def route_gates(nc, k, b_gat, ln_gamma, ln_beta):
    with ExitStack() as ctx:
        sb = lambda n, s, d: ctx.enter_context(nc.sbuf_tensor(n, s, d))
        nblk = -(-SPAN // P)
        turned_sb = sb("rg_turned", [P, nblk, BLK * RV], F32)
        r = sb("rg_r", [P, NW, RV], F32)
        con = sb("rg_con", [P, 3, RD], F32)
        t4 = sb("rg_t4", [P, NW, RH], F32)
        u4 = sb("rg_u4", [P, NW, RH], F32)
        s16 = sb("rg_s16", [P, NW, RD], F32)
        u16 = sb("rg_u16", [P, NW, RD], F32)
        one = [sb(f"rg_one{i}", [P, NW, 1], F32) for i in range(4)]
        eps = sb("rg_eps", [P, 1], F32)
        score = sb("rg_score", [P, NW, NE], F32)
        tri = sb("rg_tri", [P, NE, NE], F32)
        bank = [ctx.enter_context(nc.psum_tensor(f"rg_ps{i}", [P, 4, P], F32)) for i in range(3)]
        landed, dve, turned, evac, stored, back, a_in, a_ok = (nc.alloc_semaphore(f"rg_{n}") for n in (
            "landed", "dve", "turned", "evacuated", "stored", "back", "act_in", "act"))
        full = (SPAN // P) * P
        with nc.Block() as block:
            @block.sync
            def _(sp):
                for i, a in enumerate((b_gat, ln_gamma, ln_beta)):
                    sp.dma_start(con[:, i, :], bc(a.unsqueeze(0), [P, RD])).then_inc(landed, 16)
                sp.wait_ge(evac, 4)
                for a in range(BLK):
                    cols = slice(a * RV, (a + 1) * RV)
                    sp.dma_start(k.sums_d[a * SPAN:a * SPAN + full, :].rearrange("(k p) f -> p k f", p=P), turned_sb[:, 0:full // P, cols]).then_inc(stored, 16)
                    sp.dma_start(k.sums_d[a * SPAN + full:(a + 1) * SPAN, :], turned_sb[0:SPAN - full, full // P, cols]).then_inc(stored, 16)
                sp.wait_ge(stored, 32 * BLK)
                sp.dma_start(r[:, 0:NW - 1, :], k.sums_d[0:(NW - 1) * P, :].rearrange("(w p) f -> p w f", p=P)).then_inc(back, 16)
                sp.dma_start(r[0:TAIL, NW - 1, :], k.sums_d[(NW - 1) * P:N, :]).then_inc(back, 16)

            @block.tensor
            def _(pe):
                for b in range(nblk):
                    n = min(P, 3 * CH - b * P)
                    t = pe.transpose(bank[b // 4][0:n, b % 4, 0:BLK * RV], k.sums[:, b * P:b * P + n], k.ident[0:BLK * RV, 0:BLK * RV])
                t.then_inc(turned, 1)

            @block.scalar
            def _(act):
                def step(n, out, in_, f, **kw):
                    act.wait_ge(a_in, n)
                    act.activation(out, in_, f, **kw).then_inc(a_ok, 1)
                step(1, u4[:, :, :], t4[:, :, :], ACT.Exp)
                step(2, one[2][:, :, :], one[1][:, :, :], ACT.Sqrt, bias=eps[:, :])
                step(3, u4[:, :, :], t4[:, :, :], ACT.Exp)

            @block.vector
            def _(v):
                d = Count(dve)
                wait = lambda: v.wait_ge(dve, d.n)

                def on(ins):
                    d.on(ins)
                    wait()

                def tt(o, a, b, op):
                    on(v.tensor_tensor(o, a, b, op))
                on(v.memset(eps[:, :], EPS))
                on(v.memset(tri[:, :, :], 0.0))
                for i in range(1, NE):
                    on(v.memset(tri[:, i, 0:i], 1.0))
                v.memset(r[:, NW - 1, :], 1.0).then_inc(evac, 1)
                v.wait_ge(turned, 1)
                for b in range(3):
                    w = (4, 4, nblk - 8)[b]
                    n = P if b < 2 else 3 * CH - 8 * P
                    v.tensor_copy(turned_sb[0:n, 4 * b:4 * b + w, :], bank[b][0:n, 0:w, 0:BLK * RV]).then_inc(evac, 1)
                full16, full4 = [P, NW, RD], [P, NW, RH]
                he = lambda t: t.rearrange("p w (h e) -> p (w h) e", e=NE)
                flat = lambda t: t.rearrange("p w h -> p (w h)").unsqueeze(2)
                h, a_src = k.node_src[:, :, 0:RD], k.node_src[:, :, RD:RV]
                tt(u4[:, :, :], a_src, k.node_dst[:, :, 0:RH], ALU.add)
                on(v.scalar_tensor_tensor(out=t4[:, :, :], in0=u4[:, :, :], scalar=0.2, in1=u4[:, :, :], op0=ALU.mult, op1=ALU.max))
                tt(t4[:, :, :], t4[:, :, :], k.node_dst[:, :, RH:2 * RH], ALU.subtract)
                v.sem_inc(a_in, 1)
                v.wait_ge(a_ok, 1)
                on(v.tensor_copy(s16[:, :, :], h))
                tt(he(s16[:, :, :]), he(s16[:, :, :]), bc(flat(u4[:, :, :]), [P, NW * RH, NE]), ALU.mult)
                v.wait_ge(back, 32)
                tt(s16[:, :, :], s16[:, :, :], r[:, :, 0:RD], ALU.add)
                tt(t4[:, :, :], u4[:, :, :], r[:, :, RD:RV], ALU.add)
                on(v.tensor_scalar(t4[:, :, :], t4[:, :, :], 1e-16, None, ALU.add))
                on(v.reciprocal(u4[:, :, :], t4[:, :, :]))
                tt(he(s16[:, :, :]), he(s16[:, :, :]), bc(flat(u4[:, :, :]), [P, NW * RH, NE]), ALU.mult)
                v.wait_ge(landed, 48)
                tt(s16[:, :, :], s16[:, :, :], bc(con[:, 0:1, :], full16), ALU.add)
                on(v.reduce_sum(one[0][:, :, :], s16[:, :, :], AX.X))
                on(v.tensor_scalar(one[0][:, :, :], one[0][:, :, :], 1.0 / RD, None, ALU.mult))
                tt(s16[:, :, :], s16[:, :, :], bc(one[0][:, :, :], full16), ALU.subtract)
                tt(u16[:, :, :], s16[:, :, :], s16[:, :, :], ALU.mult)
                on(v.reduce_sum(one[1][:, :, :], u16[:, :, :], AX.X))
                on(v.tensor_scalar(one[1][:, :, :], one[1][:, :, :], 1.0 / RD, None, ALU.mult))
                v.sem_inc(a_in, 1)
                v.wait_ge(a_ok, 2)
                on(v.reciprocal(one[3][:, :, :], one[2][:, :, :]))
                tt(s16[:, :, :], s16[:, :, :], bc(one[3][:, :, :], full16), ALU.mult)
                tt(s16[:, :, :], s16[:, :, :], bc(con[:, 1:2, :], full16), ALU.mult)
                tt(s16[:, :, :], s16[:, :, :], bc(con[:, 2:3, :], full16), ALU.add)
                on(v.reduce_sum(score[:, :, :], s16[:, :, :].rearrange("p w (h e) -> p w e h", e=NE), AX.X))
                on(v.tensor_scalar(score[:, :, :], score[:, :, :], 1.0 / RH, None, ALU.mult))
                on(v.memset(t4[:, :, :], 0.0))
                for j in range(NE):
                    sj = bc(score[:, :, j:j + 1], full4)
                    tt(u4[:, :, :], sj, score[:, :, :], ALU.is_gt)
                    tt(t4[:, :, :], t4[:, :, :], u4[:, :, :], ALU.add)
                    tt(u4[:, :, :], sj, score[:, :, :], ALU.is_equal)
                    tt(u4[:, :, :], u4[:, :, :], bc(tri[:, :, j].unsqueeze(1), full4), ALU.mult)
                    tt(t4[:, :, :], t4[:, :, :], u4[:, :, :], ALU.add)
                on(v.tensor_scalar(s16[:, :, 0:NE], t4[:, :, :], 1.5, None, ALU.is_lt))
                on(v.tensor_reduce(one[0][:, :, :], score[:, :, :], AX.X, ALU.max))
                tt(t4[:, :, :], score[:, :, :], bc(one[0][:, :, :], full4), ALU.subtract)
                v.sem_inc(a_in, 1)
                v.wait_ge(a_ok, 3)
                tt(u4[:, :, :], u4[:, :, :], s16[:, :, 0:NE], ALU.mult)
                on(v.reduce_sum(one[1][:, :, :], u4[:, :, :], AX.X))
                on(v.reciprocal(one[2][:, :, :], one[1][:, :, :]))
                tt(k.gates[:, :, :], u4[:, :, :], bc(one[2][:, :, :], full4), ALU.mult)


def experts(nc, k, w1, b1, w2, b2, out):
    with ExitStack() as ctx:
        sb = lambda n, s, d: ctx.enter_context(nc.sbuf_tensor(n, s, d))
        FT = FF // P
        w1_sb = sb("ex_w1", [P, NE, 2, FF], F32)
        w2_sb = sb("ex_w2", [P, NE, FT, D], F32)
        b1_sb = sb("ex_b1", [P, NE, FT], F32)
        b2_sb = sb("ex_b2", [P, NE, D], F32)
        hid = [sb(f"ex_hid{i}", [P, FT, CN], F32) for i in range(2)]
        o = [sb(f"ex_o{i}", [P, CW, D], F32) for i in range(2)]
        h_ps = [ctx.enter_context(nc.psum_tensor(f"ex_h{i}", [P, 512], F32)) for i in range(4)]
        y_ps = [ctx.enter_context(nc.psum_tensor(f"ex_y{i}", [P, 512], F32)) for i in range(4)]
        landed, h_ok, gelu, y_ok, added, biased = (nc.alloc_semaphore(f"ex_{n}") for n in ("landed", "h", "gelu", "y", "added", "biased"))
        x_in = [nc.alloc_semaphore(f"ex_x{i}") for i in range(2)]
        stored = [nc.alloc_semaphore(f"ex_stored{i}") for i in range(2)]
        half, HALFN = NB // 2, CN // 2
        HT = 2 * FT
        YT = CW
        with nc.Block() as block:
            @block.sync
            def _(sp):
                sp.dma_start(w1_sb[:, :, :, :], w1.rearrange("e (c p) n -> p e c n", p=P)).then_inc(landed, 16)
                sp.dma_start(w2_sb[:, :, :, :], w2.rearrange("e (f p) n -> p e f n", p=P)).then_inc(landed, 16)
                sp.dma_start(b1_sb[:, :, :], b1.rearrange("e (f p) -> p e f", p=P), allow_slow_non_contiguous=True).then_inc(landed, 16)
                sp.dma_start(b2_sb[:, :, :], bc(b2.unsqueeze(0), [P, NE, D])).then_inc(landed, 16)

                def load(i, s):
                    sp.dma_start(o[s][:, :, :], k.x2_d[bass.ds(i * CN, CN), :].rearrange("(w p) f -> p w f", p=P)).then_inc(x_in[s], 16)

                def turn(j, s, load_next, last=False):
                    i = j * 2 + s
                    sp.wait_ge(added, (i + 1) * (NE * YT))
                    if last:
                        sp.dma_start(out[(NB - 1) * CN:(NW - 1) * P, :].rearrange("(w p) f -> p w f", p=P), o[s][:, 0:CW - 1, :]).then_inc(stored[s], 16)
                        sp.dma_start(out[(NW - 1) * P:N, :], o[s][0:TAIL, CW - 1, :]).then_inc(stored[s], 16)
                    else:
                        sp.dma_start(out[bass.ds(i * CN, CN), :].rearrange("(w p) f -> p w f", p=P), o[s][:, :, :]).then_inc(stored[s], 16)
                        if load_next:
                            sp.wait_ge(stored[s], (j + 1) * 16)
                            load(i + 2, s)
                load(0, 0)
                load(1, 1)
                with sp.Fori(0, half - 1) as j:
                    turn(j, 0, True)
                    turn(j, 1, True)
                turn(half - 1, 0, True)
                turn(half - 1, 1, False)
                turn(half, 0, False, True)
                sp.wait_ge(stored[0], 16 * (half + 2))
                sp.wait_ge(stored[1], 16 * half)

            @block.tensor
            def _(pe):
                pe.wait_ge(landed, 64)

                def hidden(i, e, first):
                    u = i * NE + e
                    for f in range(FT):
                        for q in range(2):
                            n = f * 2 + q
                            if not first or n >= 4:
                                pe.wait_ge(gelu, u * HT + (n - 3))
                            for c in range(2):
                                m = pe.matmul(h_ps[n % 4][:, 0:HALFN], w1_sb[:, e, c, f * P:(f + 1) * P],
                                              k.xT[:, c, bass.ds(i * CN + q * HALFN, HALFN)], start=(c == 0), stop=(c == 1))
                            m.then_inc(h_ok, 1)

                def turn(j, s, first, last):
                    i = j * 2 + s
                    for e in range(NE):
                        if e + 1 < NE:
                            hidden(i, e + 1, False)
                        elif not last:
                            hidden(i + 1, 0, False)
                        u = i * NE + e
                        pe.wait_ge(gelu, (u + 1) * HT)
                        for w in range(CW):
                            n = e * YT + w
                            if not (first and s == 0 and n < 4):
                                pe.wait_ge(added, i * (NE * YT) + (n - 3))
                            for f in range(FT):
                                m = pe.matmul(y_ps[n % 4][:, 0:D], hid[e % 2][:, f, w * P:(w + 1) * P], w2_sb[:, e, f, :],
                                              start=(f == 0), stop=(f == FT - 1))
                            m.then_inc(y_ok, 1)
                hidden(0, 0, True)
                pairs(pe, half, turn)

            @block.scalar
            def _(act):
                act.wait_ge(landed, 64)

                def turn(j, s, first, last):
                    i = j * 2 + s
                    for e in range(NE):
                        u = i * NE + e
                        if not (first and s == 0 and e < 2):
                            act.wait_ge(y_ok, (u - 1) * YT)
                        for n in range(HT):
                            f, q = n // 2, n % 2
                            act.wait_ge(h_ok, u * HT + n + 1)
                            act.activation(hid[e % 2][:, f, q * HALFN:(q + 1) * HALFN], h_ps[n % 4][:, 0:HALFN], ACT.Gelu,
                                           bias=b1_sb[:, e, f:f + 1]).then_inc(gelu, 1)
                pairs(act, half, turn)

            @block.vector
            def _(v):
                v.wait_ge(landed, 64)

                def turn(j, s, first, last):
                    i = j * 2 + s
                    gate = lambda w, e: k.gates[:, bass.ds(i * CW + w, 1), e:e + 1].rearrange("p a b -> p (a b)")
                    v.wait_ge(x_in[s], (j + 1) * 16)
                    for e in range(NE):
                        if not (first and s == 0 and e == 0):
                            v.wait_ge(biased, (i * NE + e) * CW)
                        for w in range(CW):
                            v.scalar_tensor_tensor(out=o[s][:, w, :], in0=b2_sb[:, e, :], scalar=gate(w, e), in1=o[s][:, w, :],
                                                   op0=ALU.mult, op1=ALU.add).then_inc(biased, 1)
                    v.wait_ge(biased, (i + 1) * (NE * CW))
                    for e in range(NE):
                        for w in range(CW):
                            n = e * YT + w
                            v.wait_ge(y_ok, i * (NE * YT) + n + 1)
                            if e:
                                v.wait_ge(added, i * (NE * YT) + (n - YT + 1))
                            v.scalar_tensor_tensor(out=o[s][:, w, :], in0=y_ps[n % 4][:, 0:D], scalar=gate(w, e), in1=o[s][:, w, :],
                                                   op0=ALU.mult, op1=ALU.add).then_inc(added, 1)
                pairs(v, half, turn)


class Store:
    pass


def graph_layers(nc, x, src, dst, Wq, bq, Wk, bk, Wv, bv, Wskip, bskip, gamma, beta,
                 W_gat, att_src, att_dst, b_gat, ln_gamma, ln_beta, W1, b1, W2, b2, edge_index, out):
    k = Store()
    dram = lambda n, s: nc.dram_tensor(n, s, F32).ap()
    k.reset_d = dram("reset_d", (KROW * P, HEADS, P))
    k.kv_d = dram("kv_d", (NPAD, 2 * D))
    k.xs_d = dram("xs_d", (NPAD, 3 * D))
    k.x2_d = dram("x2_d", (NPAD, D))
    k.src_tab_d = dram("src_tab_d", (NPAD, RV))
    k.dst_tab_d = dram("dst_tab_d", (NPAD, 2 * RH))
    k.sums_d = dram("sums_d", (BLK * SPAN, RV))
    with ExitStack() as whole:
        sb = lambda ctx, n, s, d: ctx.enter_context(nc.sbuf_tensor(n, s, d))
        k.ident = sb(whole, "ident", [P, P], F32)
        k.gates = sb(whole, "gates", [P, NW, NE], F32)
        k.acc = sb(whole, "acc", [P, NW, HEADS * HW], F32)
        with ExitStack() as walk:
            k.ident_b = sb(walk, "ident_b", [P, P], BF16)
            k.negbig = sb(walk, "negbig", [P, HEADS], BF16)
            k.ones_b = sb(walk, "ones_b", [P, P], BF16)
            k.iota_b = sb(walk, "iota_b", [P, P], BF16)
            k.src_i = sb(walk, "src_i", [P, NT], I32)
            k.dst_f = sb(walk, "dst_f", [P, NT], F32)
            k.last_b = sb(walk, "last_b", [P, NT], BF16)
            k.wbase = sb(walk, "wbase", [P, NS], F32)
            k.w_tab = sb(walk, "w_tab", [1, NS], I32)
            k.g_tab = sb(walk, "g_tab", [1, NS], I32)
            k.m_all = sb(walk, "m_all", [P, NW, HEADS], F32)
            edge_tables(nc, k, src, dst)
            k.q3 = sb(walk, "q3", [P, NW, 3 * D], BF16)
            project(nc, k, x, (Wk, Wv, Wq, Wskip), (bk, bv, bq, bskip))
            attend(nc, k)
        k.xT = sb(whole, "xT", [P, 2, NPAD], F32)
        with ExitStack() as route:
            k.node_src = sb(route, "node_src", [P, NW, RV], F32)
            k.node_dst = sb(route, "node_dst", [P, NW, 2 * RH], F32)
            with ExitStack() as ctx:
                k.hT = sb(ctx, "hT", [RD, NPAD], F32)
                node_update(nc, k, gamma, beta, W_gat)
                k.ends = sb(ctx, "route_ends", [P, RSTEPS, 2, RG], I32)
                k.column = sb(ctx, "column", [P, RT], F32)
                k.block_oh = sb(ctx, "block_oh", [P, RT, BLK], BF16)
                k.iota_span = sb(ctx, "iota_span", [P, 3 * CH], F16)
                k.sums = sb(ctx, "sums", [BLK * RV, 3 * CH], F32)
                route_tables(nc, k, edge_index, att_src, att_dst)
                route_edges(nc, k)
                route_gates(nc, k, b_gat, ln_gamma, ln_beta)
        experts(nc, k, W1, b1, W2, b2, out)


_INS = ["x", "src", "dst"] + ["L0_gnn_" + n for n in ("Wq", "bq", "Wk", "bk", "Wv", "bv", "Wskip", "bskip", "gamma", "beta")] \
    + ["L0_ffn_" + n for n in ("W_gat", "att_src", "att_dst", "b_gat", "ln_gamma", "ln_beta", "W1", "b1", "W2", "b2", "edge_index")]


def kernel(**inputs):
    import numpy as _np
    import concourse.bacc as _bacc
    from concourse.bass_utils import run_bass_kernel_spmd as _run

    nc = _bacc.Bacc("TRN2", target_bir_lowering=False, num_devices=1)
    arrays, args = {}, []
    for name in _INS:
        a = _np.ascontiguousarray(inputs[name])
        arrays[f"in_{name}_dram"] = a
        args.append(nc.dram_tensor(f"in_{name}_dram", a.shape, mybir.dt.from_np(a.dtype), kind="ExternalInput").ap())
    args.append(nc.dram_tensor("out_0_dram", (N, D), F32, kind="ExternalOutput").ap())
    graph_layers(nc, *args)
    r = _run(nc, [arrays], core_ids=[0])
    return r.results[0]["out_0_dram"]
```

```python
from contextlib import ExitStack

import concourse.bass as bass
from concourse import mybir

F32 = mybir.dt.float32
I32 = mybir.dt.int32
BF16 = mybir.dt.bfloat16
F16 = mybir.dt.float16
ALU = mybir.AluOpType
ACT = mybir.ActivationFunctionType
AX = mybir.AxisListType

P = 128
N, D = 6250, 256
NW = -(-N // P)
NPAD = NW * P
TAIL = N - (NW - 1) * P
HEADS = 8
DH = D // HEADS
HW = DH + 1
E = 200000
G = 4
NG = -(-E // (G * P))
NT = NG * G
KROW = -(-NT // P)
STEPS = NG + NW - 1
LOOP = 6
RUN = 1 + LOOP * (-(-(STEPS - 1) // LOOP))
AHEAD = 4
LOADS = RUN + LOOP - 1
NS = RUN + 2 * LOOP - 1
TG = G * HEADS
BIG = float(2.0 ** 100)
SCALE = float(DH) ** -0.5
EPS = 1e-5
PAD_DST = 8192

RE = 131072
RH, NE = 4, 4
RD = RH * NE
RV = RD + RH
RT = RE // P
RG = 8
RSTEPS = RT // RG
BLK = 6
SPAN = -(-N // BLK)
CH = 348
FF = 512
CW = 7
NB = NW // CW
CN = CW * P


class Count:

    def __init__(self, sem):
        self.sem, self.n = sem, 0

    def on(self, ins, by=1):
        self.n += by
        return ins.then_inc(self.sem, by)


def bc(ap, shape):
    return ap.broadcast_to(shape)


def edge_tables(nc, k, src, dst):
    with ExitStack() as ctx:
        sb = lambda n, s, d: ctx.enter_context(nc.sbuf_tensor(n, s, d))
        src_row = sb("src_row", [P, KROW, P], I32)
        dst_row = sb("dst_row", [P, KROW, P], I32)
        srcf_row = sb("srcf_row", [P, KROW, P], F32)
        dstf_row = sb("dstf_row", [P, KROW, P], F32)
        last_row = sb("last_row", [P, KROW, P], F32)
        reset_row = sb("reset_row", [P, KROW, P], F32)
        differs = sb("differs", [P, KROW, P - 1], F32)
        ends = sb("ends", [P, P], F32)
        threshold = sb("threshold", [P, 1], F32)
        part = sb("part", [P, 1], F32)
        steps = sb("steps", [P, NS], F32)
        below = sb("below", [P, NG], F32)
        event = sb("event", [P, 2], F32)
        passed = sb("passed", [P, NS], F32)
        ones = sb("ones", [P, P], F32)
        wstep = sb("wstep", [P, NS], F32)
        gstep = sb("gstep", [P, NS], F32)
        bank = [ctx.enter_context(nc.psum_tensor(f"et{i}", [P, 512], F32)) for i in range(4)]
        padded, landed, dve, turned, evac, stored, made, mm = (
            nc.alloc_semaphore(n) for n in ("et_padded", "et_landed", "et_dve", "et_turned", "et_evacuated",
                                            "et_stored", "et_constants", "et_products"))
        full = E // P - P * (KROW - 1)
        rest = E % P
        e0 = P * P * (KROW - 1)
        with nc.Block() as block:
            @block.sync
            def _(sp):
                for a, row in ((src, src_row), (dst, dst_row)):
                    sp.dma_start(row[:, 0:KROW - 1, :], a[0:e0].rearrange("(k r p) -> r k p", r=P, p=P)).then_inc(landed, 16)
                sp.wait_ge(padded, 2)
                for a, row in ((src, src_row), (dst, dst_row)):
                    sp.dma_start(row[0:full, KROW - 1, :], a[e0:e0 + full * P].rearrange("(r p) -> r p", p=P)).then_inc(landed, 16)
                    sp.dma_start(row[full:full + 1, KROW - 1, 0:rest], a[e0 + full * P:E].rearrange("(r p) -> r p", r=1)).then_inc(landed, 16)
                sp.wait_ge(dve, 6)
                for b in range(KROW):
                    sp.dma_start(k.reset_d[P * b:P * (b + 1), :, :], bc(reset_row[:, b:b + 1, :], [P, HEADS, P])).then_inc(stored, 16)
                sp.wait_ge(stored, 16 * KROW)

            @block.gpsimd
            def _(pool):
                pool.memset(k.ident[:, :], 0.0).then_inc(made, 1)
                pool.memset(ones[:, :], 1.0).then_inc(made, 1)
                pool.memset(k.one[:, :], 1.0)
                pool.memset(k.negbig[:, :], -BIG / P).then_inc(made, 1)
                pool.memset(k.ones_b[:, :], 1.0).then_inc(made, 1)
                pool.iota(k.iota_b[:, :], [[1, P]], base=0, channel_multiplier=0, allow_small_or_imprecise_dtypes=True).then_inc(made, 1)
                pool.iota(threshold[:, :], [[0, 1]], base=P, channel_multiplier=P, allow_small_or_imprecise_dtypes=True).then_inc(made, 1)
                pool.iota(part[:, :], [[0, 1]], base=0, channel_multiplier=1, allow_small_or_imprecise_dtypes=True).then_inc(made, 1)
                pool.iota(steps[:, :], [[1, NS]], base=0, channel_multiplier=0, allow_small_or_imprecise_dtypes=True).then_inc(made, 1)
                pool.wait_ge(made, 8)
                pool.affine_select(out=k.ident[:, :], in_=k.ident[:, :], compare_op=ALU.not_equal, fill=1.0,
                                   base=0, pattern=[[-1, P]], channel_multiplier=1).then_inc(made, 1)

            @block.vector
            def _(v):
                d = Count(dve)
                v.memset(src_row[:, KROW - 1, :], 0).then_inc(padded, 1)
                v.memset(dst_row[:, KROW - 1, :], PAD_DST).then_inc(padded, 1)
                v.wait_ge(landed, 96)
                d.on(v.tensor_copy(dstf_row[:, :, :], dst_row[:, :, :]))
                d.on(v.tensor_copy(srcf_row[:, :, :], src_row[:, :, :]))
                v.wait_ge(dve, 1)
                d.on(v.tensor_tensor(differs[:, :, :], dstf_row[:, :, 0:P - 1], dstf_row[:, :, 1:P], ALU.not_equal))
                d.on(v.memset(reset_row[:, :, 0:1], 0.0))
                d.on(v.memset(last_row[:, :, P - 1:P], BIG))
                v.wait_ge(dve, 3)
                d.on(v.tensor_scalar(reset_row[:, :, 1:P], differs[:, :, :], -BIG, None, ALU.mult))
                d.on(v.tensor_scalar(last_row[:, :, 0:P - 1], differs[:, :, :], BIG, None, ALU.mult))
                v.wait_ge(made, 9)
                v.tensor_copy(k.ident_b[:, :], k.ident[:, :]).then_inc(made, 1)
                d.on(v.tensor_copy(ends[:, :], bc(k.ident[:, P - 1:P], [P, P])))
                for b in range(KROW):
                    n = min(P, NT - P * b)
                    at = slice(P * b, P * b + n)
                    ps = bank[b % 2]
                    v.wait_ge(turned, b + 1)
                    v.tensor_copy(k.src_i[:, at], ps[:, 0:n])
                    v.tensor_copy(k.dst_f[:, at], ps[:, P:P + n])
                    v.tensor_copy(k.last_b[:, at], ps[:, 2 * P:2 * P + n]).then_inc(evac, 1)
                v.wait_ge(mm, 1)
                d.on(v.tensor_scalar(below[:, :], bank[2][:, 0:NG], threshold[:, :], None, ALU.is_lt))
                v.wait_ge(dve, d.n)
                d.on(v.reduce_sum(event[:, 0:1], below[:, :], AX.X))
                v.wait_ge(dve, d.n)
                d.on(v.tensor_tensor(event[:, 1:2], event[:, 0:1], part[:, :], ALU.add))
                v.wait_ge(dve, d.n)
                d.on(v.tensor_scalar(passed[:, :], steps[:, :], event[:, 1:2], None, ALU.is_gt))
                v.wait_ge(mm, 2)
                d.on(v.tensor_scalar(wstep[:, :], bank[3][:, 0:NS], float(NW - 1), None, ALU.min))
                v.wait_ge(dve, d.n)
                d.on(v.tensor_tensor(gstep[:, :], steps[:, :], wstep[:, :], ALU.subtract))
                d.on(v.tensor_scalar(k.wbase[:, :], wstep[:, :], float(P), None, ALU.mult))
                v.wait_ge(dve, d.n)
                d.on(v.memset(k.wbase[:, STEPS:NS], 1.0e6))
                v.tensor_copy(k.w_tab[:, :], wstep[0:1, :])
                d.on(v.tensor_scalar(k.g_tab[:, :], gstep[0:1, :], float(NG - 1), float(G), ALU.min, ALU.mult))

            @block.tensor
            def _(pe):
                pe.wait_ge(made, 9)
                pe.wait_ge(dve, 7)
                for b in range(KROW):
                    if b >= 2:
                        pe.wait_ge(evac, b - 1)
                    for j, row in enumerate((srcf_row, dstf_row, last_row)):
                        t = pe.transpose(bank[b % 2][:, j * P:(j + 1) * P], row[:, b, :], k.ident[:, :])
                    t.then_inc(turned, 1)
                pe.wait_ge(evac, KROW)
                pe.wait_ge(dve, 8)
                pe.matmul(bank[2][:, 0:NG], ends[:, :], k.dst_f[:, G - 1:NT:G], start=True, stop=True).then_inc(mm, 1)
                pe.wait_ge(dve, 12)
                pe.matmul(bank[3][:, 0:NS], ones[:, :], passed[:, :], start=True, stop=True).then_inc(mm, 1)


class Step:

    def __init__(self, base, offset):
        self.base, self.offset = base, offset

    def __add__(self, n):
        return Step(self.base, self.offset + n)

    @property
    def v(self):
        return self.base * LOOP + self.offset

    @property
    def slot(self):
        return self.offset % LOOP

    @property
    def turn(self):
        return self.base + self.offset // LOOP

    def from_(self, n):
        return self.v >= n if isinstance(self.base, int) else self.offset + LOOP >= n


def project(nc, k, x, wts, biases):
    with ExitStack() as ctx:
        sb = lambda n, s, d: ctx.enter_context(nc.sbuf_tensor(n, s, d))
        ps = lambda n, s, d: ctx.enter_context(nc.psum_tensor(n, s, d))
        x_sb = k.acc[:, :, 0:D]
        stats = sb("stats", [P, NW, 6], F32)
        mean_var = sb("mean_var", [P, NW, 2], F32)
        rstd = sb("rstd", [P, NW], F32)
        eps = sb("eps", [P, 1], F32)
        w_sb = sb("w_sb", [P, 2, 4 * D], F32)
        b_sb = sb("b_sb", [P, 4 * D], F32)
        xs = [sb(f"xs{i}", [P, 2 * D], F32) for i in range(LOOP)]
        kv = [sb(f"kv{i}", [P, 2 * D], F32) for i in range(LOOP)]
        q3 = [sb(f"pq3_{i}", [P, 3 * D], BF16) for i in range(LOOP)]
        xt = [sb(f"xt{i}", [P, 2, P], F32) for i in range(2)]
        qf = sb("qf", [P, D], F32)
        resid = sb("resid", [P, D], F32)
        xt_ps = [ps(f"xt_ps{i}", [P, 2, P], F32) for i in range(2)]
        kv_ps = [ps(f"kv_ps{i}", [P, 512], F32) for i in range(2)]
        qs_ps = [ps(f"qs_ps{i}", [P, 512], F32) for i in range(2)]
        names = ("landed", "padded", "stats", "aggr", "sqrt", "rstd", "xn", "turned", "xt",
                 "products", "q", "hi", "resid", "mid", "lo", "kv", "skip", "xstored", "split_seen")
        ok = {n: nc.alloc_semaphore(f"pr_{n}") for n in names}
        kv_stored, xs_stored, q3_stored = ([nc.alloc_semaphore(f"pr_{n}_stored{i}") for i in range(LOOP)] for n in ("kv", "xs", "q3"))
        LAST = (NW - 1) // LOOP

        def windows(eng, body):
            for i in range(LOOP):
                body(Step(0, i), False)
            with eng.Fori(1, LAST) as j:
                for c in range(LOOP):
                    body(Step(j, c), False)
            body(Step(LAST, 0), True)

        with nc.Block() as block:
            @block.sync
            def _(sp):
                sp.wait_ge(ok["padded"], 1)
                sp.dma_start(x_sb[:, 0:NW - 1, :], x[0:(NW - 1) * P, :].rearrange("(w p) f -> p w f", p=P)).then_inc(ok["landed"], 16)
                sp.dma_start(x_sb[0:TAIL, NW - 1, :], x[(NW - 1) * P:N, :]).then_inc(ok["landed"], 16)
                for i in range(4):
                    sp.dma_start(w_sb[:, :, i * D:(i + 1) * D], wts[i].rearrange("(c p) n -> p c n", p=P)).then_inc(ok["landed"], 16)
                    sp.dma_start(b_sb[:, i * D:(i + 1) * D], bc(biases[i].unsqueeze(0), [P, D])).then_inc(ok["landed"], 16)
                sp.wait_ge(ok["landed"], 160)
                sp.dma_start(k.xs_d[:, 2 * D:3 * D].rearrange("(w p) f -> p w f", p=P), x_sb[:, :, :]).then_inc(ok["xstored"], 16)

                def store(s, last):
                    rows = bass.ds(s.v * P, P)
                    sp.wait_ge(ok["kv"], s.v + 1)
                    sp.dma_start(k.kv_d[rows, :], kv[s.slot][:, :]).then_inc(kv_stored[s.slot], 16)
                    sp.wait_ge(ok["skip"], s.v + 1)
                    sp.dma_start(k.xs_d[rows, 0:2 * D], xs[s.slot][:, :]).then_inc(xs_stored[s.slot], 16)
                    sp.wait_ge(ok["lo"], s.v + 1)
                    sp.sem_inc(ok["split_seen"], 1)
                    sp.dma_start(k.q3_d[rows, :], q3[s.slot][:, :]).then_inc(q3_stored[s.slot], 16)
                windows(sp, store)
                sp.wait_ge(ok["xstored"], 16)
                for i in range(LOOP):
                    for stored in (kv_stored, xs_stored, q3_stored):
                        sp.wait_ge(stored[i], 16 * (LAST + (i == 0)))

            @block.scalar
            def _(act):
                act.wait_ge(ok["aggr"], 1)
                act.activation(rstd[:, :], mean_var[:, :, 1], ACT.Sqrt, bias=eps[:, :]).then_inc(ok["sqrt"], 1)

                def copy(s, last):
                    act.wait_ge(ok["turned"], s.v + 1)
                    if s.from_(2):
                        act.wait_ge(ok["products"], s.v - 1)
                    act.copy(xt[s.offset % 2][:, :, :], xt_ps[s.offset % 2][:, :, :]).then_inc(ok["xt"], 1)
                windows(act, copy)

            @block.tensor
            def _(pe):
                pe.wait_ge(ok["landed"], 160)

                def turn(s):
                    pe.wait_ge(ok["xn"], s.v + 1)
                    if s.from_(2):
                        pe.wait_ge(ok["xt"], s.v - 1)
                    for c in range(2):
                        t = pe.transpose(xt_ps[s.offset % 2][:, c, :], xs[s.slot][:, c * P:(c + 1) * P], k.ident[:, :])
                    t.then_inc(ok["turned"], 1)

                def products(s, last):
                    if not last:
                        turn(s + 1)
                    p = s.offset % 2
                    pe.wait_ge(ok["xt"], s.v + 1)
                    if s.from_(2):
                        pe.wait_ge(ok["skip"], s.v - 1)
                    for bank, at in ((kv_ps[p], 0), (qs_ps[p], 2 * D)):
                        for c in range(2):
                            m = pe.matmul(bank[:, :], xt[p][:, c, :], w_sb[:, c, at:at + 2 * D], start=(c == 0), stop=(c == 1))
                    m.then_inc(ok["products"], 1)
                turn(Step(0, 0))
                windows(pe, products)

            @block.vector
            def _(v):
                v.memset(x_sb[:, NW - 1, :], 0.0).then_inc(ok["padded"], 1)
                v.memset(eps[:, :], EPS)
                v.wait_ge(ok["landed"], 160)
                with v.Fori(0, NW) as i:
                    v.bn_stats(stats[:, bass.ds(i, 1), :], x_sb[:, bass.ds(i, 1), :]).then_inc(ok["stats"], 1)
                v.wait_ge(ok["stats"], NW)
                for i in range(NW):
                    a = v.bn_aggr(mean_var[:, i, :], stats[:, i, :])
                a.then_inc(ok["aggr"], 1)
                v.wait_ge(ok["sqrt"], 1)
                v.reciprocal(rstd[:, :], rstd[:, :]).then_inc(ok["rstd"], 1)
                v.wait_ge(ok["rstd"], 1)

                def normalise(s):
                    if s.from_(LOOP):
                        v.wait_ge(xs_stored[s.slot], s.turn * 16)
                    v.tensor_scalar(xs[s.slot][:, 0:D], x_sb[:, bass.ds(s.v, 1), :].rearrange("p a f -> p (a f)"),
                                    mean_var[:, bass.ds(s.v, 1), 0:1].rearrange("p a f -> p (a f)"), rstd[:, bass.ds(s.v, 1)],
                                    ALU.subtract, ALU.mult).then_inc(ok["xn"], 1)

                def evacuate(s, last):
                    p, split = s.offset % 2, q3[s.slot]
                    v.wait_ge(ok["products"], s.v + 1)
                    if s.from_(LOOP):
                        v.wait_ge(kv_stored[s.slot], s.turn * 16)
                        v.wait_ge(q3_stored[s.slot], s.turn * 16)
                    v.tensor_tensor(qf[:, :], qs_ps[p][:, 0:D], b_sb[:, 2 * D:3 * D], ALU.add).then_inc(ok["q"], 1)
                    v.tensor_tensor(kv[s.slot][:, :], kv_ps[p][:, :], b_sb[:, 0:2 * D], ALU.add).then_inc(ok["kv"], 1)
                    v.wait_ge(ok["q"], s.v + 1)
                    v.tensor_copy(split[:, 0:D], qf[:, :]).then_inc(ok["hi"], 1)
                    v.tensor_tensor(xs[s.slot][:, D:2 * D], qs_ps[p][:, D:2 * D], b_sb[:, 3 * D:4 * D], ALU.add).then_inc(ok["skip"], 1)
                    v.wait_ge(ok["hi"], s.v + 1)
                    v.tensor_tensor(resid[:, :], qf[:, :], split[:, 0:D], ALU.subtract).then_inc(ok["resid"], 1)
                    if not last:
                        normalise(s + 2)
                    v.wait_ge(ok["resid"], s.v + 1)
                    v.tensor_copy(split[:, D:2 * D], resid[:, :]).then_inc(ok["mid"], 1)
                    v.wait_ge(ok["mid"], s.v + 1)
                    v.tensor_tensor(split[:, 2 * D:3 * D], resid[:, :], split[:, D:2 * D], ALU.subtract).then_inc(ok["lo"], 1)
                normalise(Step(0, 0))
                normalise(Step(0, 1))
                for i in range(LOOP):
                    evacuate(Step(0, i), False)
                with v.Fori(1, LAST - 1) as j:
                    for c in range(LOOP):
                        evacuate(Step(j, c), False)
                for c in range(LOOP):
                    evacuate(Step(LAST - 1, c), c == LOOP - 1)
                evacuate(Step(LAST, 0), True)


def attend(nc, k):
    with ExitStack() as ctx:
        sb = lambda n, s, d: ctx.enter_context(nc.sbuf_tensor(n, s, d))
        ps = lambda n, s, d: ctx.enter_context(nc.psum_tensor(n, s, d))
        KV = [sb(f"KV{i}", [P, G, 2 * D], F32) for i in range(LOOP)]
        idx = [sb(f"idx{i}", [P, G], I32) for i in range(LOOP)]
        off = [sb(f"off{i}", [P, G], F32) for i in range(LOOP)]
        square = sb("square", [P, G, P], BF16)
        oh = [sb(f"oh{i}", [P, G, P], BF16) for i in range(LOOP)]
        ohT = [sb(f"ohT{i}", [P, G, P], BF16) for i in range(LOOP)]
        oh32 = [sb(f"oh32_{i}", [P, G, P], F32) for i in range(2)]
        reset = [sb(f"reset{i}", [TG, P], F32) for i in range(LOOP)]
        q3 = [sb(f"q3_{i}", [P, 3 * D], BF16) for i in range(LOOP)]
        prod = sb("prod", [P, G, D], F32)
        lg = [sb(f"lg{i}", [P, TG], F32) for i in range(LOOP)]
        running = sb("running", [TG, P], F32)
        seg_max = sb("seg_max", [P, G, HEADS], BF16)
        tile_max = sb("tile_max", [P, HEADS], F32)
        m_new = sb("m_new", [P, HEADS], BF16)
        m_fall = sb("m_fall", [P, HEADS], F32)
        fac = [sb(f"fac{i}", [P, HEADS], F32) for i in range(2)]
        dl = sb("dl", [P, TG], F32)
        msg = [sb(f"msg{i}", [P, G, HEADS, HW], F32) for i in range(2)]
        Q = [ps(f"Q{i}", [P, G, D], F32) for i in range(2)]
        ohT_ps = ps("ohT_ps", [P, G, P], BF16)
        small_ps = ps("small_ps", [P, 4, P], F32)
        lgT_ps, runT_ps, ref_ps = small_ps[0:TG, 0, :], small_ps[:, 1, 0:TG], small_ps[:, 2, 0:TG]
        max_ps = ps("max_ps", [P, 512], F32)
        agg_ps = ps("agg_ps", [P, 512], F32)
        names = ("idx", "idx_seen", "off", "square", "oh", "turned", "ohT", "q", "prod", "lg", "lgT", "running", "small",
                 "seg_max", "max", "tile_max", "m_new", "m_fall", "m_all", "fac", "dl", "p", "msg", "oh32", "agg",
                 "scaled", "acc", "cleared", "resets_seen")
        ok = {n: nc.alloc_semaphore(f"at_{n}") for n in names}
        kv_landed = [nc.alloc_semaphore(f"at_kv_landed{i}") for i in range(LOOP)]
        q3_landed = [nc.alloc_semaphore(f"at_q3_landed{i}") for i in range(LOOP)]
        reset_landed = [nc.alloc_semaphore(f"at_reset_landed{i}") for i in range(LOOP)]

        def walk(eng, body):
            body(Step(0, 0), True)
            with eng.Fori(0, (RUN - 1) // LOOP) as j:
                for c in range(LOOP):
                    body(Step(j, c + 1), False)

        def load(eng, tab, s, hi):
            return eng.value_load(tab[0:1, bass.ds(s.v, 1)], min_val=0, max_val=hi)

        with nc.Block() as block:
            @block.gpsimd
            def _(pool):
                def gather(s, first):
                    if not first:
                        pool.wait_ge(ok["msg"], s.v - (LOOP - 1))
                    g = load(pool, k.g_tab, s, NT - G)
                    pool.tensor_copy(idx[s.slot][:, :], k.src_i[:, bass.ds(g, G)]).then_inc(ok["idx"], 1)
                    pool.wait_ge(ok["idx"], s.v + 1)
                    pool.sem_inc(ok["idx_seen"], 1)
                    for t in range(G):
                        pool.indirect_dma_start(out=KV[s.slot][:, t, :], out_offset=None, in_=k.kv_d,
                                                in_offset=bass.IndirectOffsetOnAxis(ap=idx[s.slot][:, t:t + 1], axis=0)
                                                ).then_inc(kv_landed[s.slot], 16)
                for i in range(LOOP):
                    gather(Step(0, i), True)
                with pool.Fori(1, LOADS // LOOP) as j:
                    for c in range(LOOP):
                        gather(Step(j, c), False)
                for s in kv_landed:
                    pool.wait_ge(s, 16 * G * (LOADS // LOOP))

            @block.sync
            def _(sp):
                def resets(s, first):
                    if not first:
                        sp.wait_ge(ok["running"], s.v - (LOOP - 1))
                        sp.sem_inc(ok["resets_seen"], 1)
                    w = load(sp, k.w_tab, s, NW - 1)
                    sp.dma_start(q3[s.slot][:, :], k.q3_d[bass.ds(w * P, P), :]).then_inc(q3_landed[s.slot], 16)
                    g = load(sp, k.g_tab, s, NT - G)
                    sp.dma_start(reset[s.slot][:, :], k.reset_d[bass.ds(g, G), :, :].rearrange("t h p -> (t h) p")
                                 ).then_inc(reset_landed[s.slot], 16)
                for i in range(LOOP):
                    resets(Step(0, i), True)
                with sp.Fori(1, LOADS // LOOP) as j:
                    for c in range(LOOP):
                        resets(Step(j, c), False)
                for s in reset_landed + q3_landed:
                    sp.wait_ge(s, 16 * (LOADS // LOOP))

            @block.vector
            def _(v):
                def offsets(s, g):
                    v.tensor_scalar(off[s.slot][:, :], k.dst_f[:, bass.ds(g, G)], -1.0, k.wbase[:, bass.ds(s.v, 1)],
                                    ALU.mult, ALU.add).then_inc(ok["off"], 1)

                def product(s):
                    v.wait_ge(kv_landed[s.slot], (s.turn + 1) * (16 * G))
                    v.wait_ge(ok["q"], s.v + 1)
                    v.tensor_tensor(prod[:, :, :], KV[s.slot][:, :, 0:D], Q[s.offset % 2][:, :, :], ALU.mult).then_inc(ok["prod"], 1)

                def logits(s):
                    v.wait_ge(ok["prod"], s.v + 1)
                    v.reduce_sum(lg[s.slot][:, :], prod[:, :, :].rearrange("p t (h d) -> p (t h) d", d=DH), AX.X
                                 ).then_inc(ok["lg"], 1)

                def scan(s):
                    v.wait_ge(ok["lgT"], s.v + 1)
                    v.wait_ge(reset_landed[s.slot], (s.turn + 1) * 16)
                    v.tensor_tensor_scan(running[:, :], reset[s.slot][:, :], lgT_ps, -BIG, ALU.add, ALU.max).then_inc(ok["running"], 1)

                def segment_max(s, g):
                    v.wait_ge(ok["small"], s.v + 1)
                    v.scalar_tensor_tensor(out=seg_max[:, :, :], in0=bc(k.last_b[:, bass.ds(g, G)].unsqueeze(2), [P, G, HEADS]),
                                           scalar=1.0 / BIG, in1=runT_ps.rearrange("p (t h) -> p t h", h=HEADS),
                                           op0=ALU.mult, op1=ALU.mult).then_inc(ok["seg_max"], 1)

                def sums(w):
                    return k.acc[:, bass.ds(w, 1), :].rearrange("p a (h e) -> p (a h) e", e=HW)

                def scale_sums(s, w):
                    v.wait_ge(ok["fac"], s.v + 1)
                    v.wait_ge(ok["acc"], s.v + 1)
                    v.tensor_tensor(sums(w), sums(w), bc(fac[s.offset % 2][:, :].unsqueeze(2), [P, HEADS, HW]), ALU.mult).then_inc(ok["scaled"], 1)

                def add_sums(s, w):
                    v.wait_ge(ok["agg"], s.v + 1)
                    v.wait_ge(ok["scaled"], s.v + 1)
                    v.tensor_tensor(sums(w), sums(w), agg_ps[:, 0:HEADS * HW].rearrange("p (h e) -> p h e", e=HW), ALU.add).then_inc(ok["acc"], 1)

                def body(s, first):
                    own = first or s.slot == 1
                    w = load(v, k.w_tab, s, NW - 1) if own else held["w"]
                    w_last = None if first else load(v, k.w_tab, s + (-1), NW - 1) if own else held["w_last"]
                    m_all = k.m_all[:, bass.ds(w, 1), :].rearrange("p a h -> p (a h)")
                    scan(s + 1)
                    v.wait_ge(ok["max"], s.v + 1)
                    v.tensor_reduce(tile_max[:, :], max_ps[:, 0:TG].rearrange("p (t h) -> p h t", h=HEADS), AX.X, ALU.max).then_inc(ok["tile_max"], 1)
                    if not first:
                        scale_sums(s + (-1), w_last)
                    v.wait_ge(ok["tile_max"], s.v + 1)
                    if not first:
                        v.wait_ge(ok["m_all"], s.v)
                    v.tensor_tensor(m_new[:, :], m_all, tile_max[:, :], ALU.max).then_inc(ok["m_new"], 1)
                    if not own:
                        offsets(s + AHEAD, held["g_ahead"])
                    v.wait_ge(ok["m_new"], s.v + 1)
                    v.tensor_tensor(m_fall[:, :], m_all, m_new[:, :], ALU.subtract).then_inc(ok["m_fall"], 1)
                    product(s + 2)
                    g = load(v, k.g_tab, s + 1, NT - G)
                    if own:
                        offsets(s + AHEAD, load(v, k.g_tab, s + AHEAD, NT - G))
                    segment_max(s + 1, g)
                    v.wait_ge(ok["m_fall"], s.v + 1)
                    v.tensor_scalar(m_all, m_new[:, :], 1.0, None, ALU.mult).then_inc(ok["m_all"], 1)
                    v.wait_ge(ok["small"], s.v + 2)
                    v.tensor_tensor(dl[:, :], lg[s.slot][:, :], ref_ps, ALU.subtract).then_inc(ok["dl"], 1)
                    logits(s + 2)
                    more = not first and s.slot != 0
                    if more:
                        held["w"], held["w_last"] = load(v, k.w_tab, s + 1, NW - 1), w
                    v.wait_ge(ok["p"], s.v + 1)
                    m = msg[s.offset % 2]
                    v.tensor_tensor(m[:, :, :, 0:DH], KV[s.slot][:, :, D:2 * D].rearrange("p t (h d) -> p t h d", d=DH),
                                    bc(m[:, :, :, DH:HW], [P, G, HEADS, DH]), ALU.mult).then_inc(ok["msg"], 1)
                    if more:
                        held["g_ahead"] = load(v, k.g_tab, s + 1 + AHEAD, NT - G)
                    if not first:
                        add_sums(s + (-1), w_last)

                held = {}
                for i in range(AHEAD):
                    offsets(Step(0, i), load(v, k.g_tab, Step(0, i), NT - G))
                v.memset(k.acc[:, :, :], 0.0).then_inc(ok["acc"], 1)
                v.memset(k.m_all[:, :, :], -BIG).then_inc(ok["cleared"], 1)
                product(Step(0, 0))
                logits(Step(0, 0))
                scan(Step(0, 0))
                segment_max(Step(0, 0), load(v, k.g_tab, Step(0, 0), NT - G))
                product(Step(0, 1))
                logits(Step(0, 1))
                v.wait_ge(ok["cleared"], 1)
                walk(v, body)
                end = Step((RUN - 1) // LOOP, 0)
                w = load(v, k.w_tab, end, NW - 1)
                scale_sums(end, w)
                add_sums(end, w)

            @block.scalar
            def _(act):
                def one_hot(s, first):
                    act.wait_ge(ok["off"], s.v + 1)
                    if not first:
                        act.wait_ge(ok["oh"], s.v)
                    for t in range(G):
                        q = act.activation(square[:, t, :], k.iota_b[:, :], ACT.Square, bias=off[s.slot][:, t:t + 1])
                    q.then_inc(ok["square"], 1)
                    act.wait_ge(ok["square"], s.v + 1)
                    act.activation(oh[s.slot][:, :, :], square[:, :, :], ACT.Relu, bias=k.one[:, :], scale=-1.0).then_inc(ok["oh"], 1)

                def turn_copy(s):
                    act.wait_ge(ok["turned"], s.v + 1)
                    act.copy(ohT[s.slot][:, :, :], ohT_ps[:, :, :]).then_inc(ok["ohT"], 1)

                def body(s, first):
                    act.wait_ge(ok["m_fall"], s.v + 1)
                    act.activation(fac[s.offset % 2][:, :], m_fall[:, :], ACT.Exp, scale=SCALE).then_inc(ok["fac"], 1)
                    one_hot(s + AHEAD, False)
                    act.wait_ge(ok["dl"], s.v + 1)
                    act.activation(msg[s.offset % 2][:, :, :, DH:HW], dl[:, :].rearrange("p (t h a) -> p t h a", h=HEADS, a=1), ACT.Exp,
                                   scale=SCALE).then_inc(ok["p"], 1)
                    act.copy(oh32[s.offset % 2][:, :, :], oh[s.slot][:, :, :]).then_inc(ok["oh32"], 1)
                    turn_copy(s + AHEAD)
                for i in range(AHEAD):
                    one_hot(Step(0, i), i == 0)
                    turn_copy(Step(0, i))
                walk(act, body)

            @block.tensor
            def _(pe):
                def turn(s):
                    pe.wait_ge(ok["oh"], s.v + 1)
                    for t in range(G):
                        m = pe.transpose(ohT_ps[:, t, :], oh[s.slot][:, t, :], k.ident_b[:, :])
                    m.then_inc(ok["turned"], 1)

                def queries(s):
                    pe.wait_ge(q3_landed[s.slot], (s.turn + 1) * 16)
                    pe.wait_ge(ok["ohT"], s.v + 1)
                    for t in range(G):
                        for c in range(3):
                            m = pe.matmul(Q[s.offset % 2][:, t, :], ohT[s.slot][:, t, :],
                                          q3[s.slot][:, c * D:(c + 1) * D],
                                          start=(c == 0), stop=(c == 2))
                    m.then_inc(ok["q"], 1)

                def turn_logits(s):
                    pe.wait_ge(ok["lg"], s.v + 1)
                    pe.transpose(lgT_ps, lg[s.slot][:, :], k.ident[:, :]).then_inc(ok["lgT"], 1)

                def maxima(s, g):
                    pe.wait_ge(ok["seg_max"], s.v + 1)
                    for t in range(G):
                        at = max_ps[:, t * HEADS:(t + 1) * HEADS]
                        pe.matmul(at, k.ones_b[:, :], k.negbig[:, 0:HEADS], start=True, stop=False)
                        pe.matmul(at, oh[s.slot][:, t, :], bc(k.last_b[:, bass.ds(g + t, 1)], [P, HEADS]), start=False, stop=False)
                        m = pe.matmul(at, oh[s.slot][:, t, :], seg_max[:, t, :], start=False, stop=True)
                    m.then_inc(ok["max"], 1)

                def sums(s):
                    pe.wait_ge(ok["oh32"], s.v + 1)
                    pe.wait_ge(ok["msg"], s.v + 1)
                    for t in range(G):
                        m = pe.matmul(agg_ps[:, 0:HEADS * HW], oh32[s.offset % 2][:, t, :],
                                      msg[s.offset % 2][:, t, :, :].rearrange("p h e -> p (h e)"), start=(t == 0), stop=(t == G - 1))
                    m.then_inc(ok["agg"], 1)

                def body(s, first):
                    pe.wait_ge(ok["m_new"], s.v + 1)
                    for t in range(G):
                        pe.matmul(ref_ps[:, t * HEADS:(t + 1) * HEADS], ohT[s.slot][:, t, :], m_new[:, :], start=True, stop=True)
                    pe.transpose(runT_ps, running[:, :], k.ident[0:TG, 0:TG]).then_inc(ok["small"], 1)
                    if not first:
                        sums(s + (-1))
                    g = load(pe, k.g_tab, s + 1, NT - G)
                    turn_logits(s + 2)
                    maxima(s + 1, g)
                    turn(s + AHEAD)
                    queries(s + 3)
                for i in range(AHEAD):
                    if i:
                        pe.wait_ge(ok["ohT"], i)
                    turn(Step(0, i))
                queries(Step(0, 0))
                queries(Step(0, 1))
                turn_logits(Step(0, 0))
                pe.wait_ge(ok["running"], 1)
                pe.transpose(runT_ps, running[:, :], k.ident[0:TG, 0:TG]).then_inc(ok["small"], 1)
                maxima(Step(0, 0), load(pe, k.g_tab, Step(0, 0), NT - G))
                queries(Step(0, 2))
                turn_logits(Step(0, 1))
                walk(pe, body)
                pe.wait_ge(ok["acc"], RUN)
                sums(Step((RUN - 1) // LOOP, 0))


def pairs(eng, half, body):
    body(0, 0, True, False)
    body(0, 1, True, False)
    with eng.Fori(1, half) as j:
        body(j, 0, False, False)
        body(j, 1, False, False)
    body(half, 0, False, True)


class Chain:

    def __init__(self, eng, sem, turn, per_turn):
        self.eng, self.sem, self.base, self.n, self.per_turn = eng, sem, turn * per_turn, 0, per_turn

    def on(self, ins):
        self.n += 1
        assert self.n <= self.per_turn
        ins.then_inc(self.sem, 1)

    def wait(self):
        self.eng.wait_ge(self.sem, self.base + self.n)

    def done(self):
        assert self.n == self.per_turn, self.n


def node_update(nc, k, gamma, beta, w_gat):
    with ExitStack() as ctx:
        sb = lambda n, s, d: ctx.enter_context(nc.sbuf_tensor(n, s, d))
        ps = lambda n, s, d: ctx.enter_context(nc.psum_tensor(n, s, d))
        xs = [sb(f"nu_xs{i}", [P, CW, 3 * D], F32) for i in range(2)]
        den = sb("nu_den", [P, CW, HEADS, 1], F32)
        out = sb("nu_out", [P, CW, D], F32)
        x2 = [sb(f"nu_x2_{i}", [P, CW, D], F32) for i in range(2)]
        xn2 = sb("nu_xn2", [P, CW, D], F32)
        gam = sb("nu_gam", [P, D], F32)
        bet = sb("nu_bet", [P, D], F32)
        wg = sb("nu_wg", [P, 2, RD], F32)
        stats = sb("nu_stats", [P, CW, 6], F32)
        mv = sb("nu_mv", [P, CW, 2], F32)
        rstd = sb("nu_rstd", [P, CW], F32)
        eps = sb("nu_eps", [P, 1], F32)
        turn_ps = [ps(f"nu_turn{i}", [P, 4, P], F32) for i in range(4)]
        h_ps = [ps(f"nu_h{i}", [RD, 512], F32) for i in range(2)]
        const, ready, dve, s_stats, s_in, s_gelu, s_var, s_sqrt, turned, xt_ok, h_ok, h_read = (
            nc.alloc_semaphore(f"nu_{n}") for n in ("constants", "eps", "dve", "stats", "preact", "gelu", "variance", "sqrt", "turned", "xT", "h", "h_read"))
        landed = [nc.alloc_semaphore(f"nu_landed{i}") for i in range(2)]
        stored = [nc.alloc_semaphore(f"nu_stored{i}") for i in range(2)]
        half, K = NB // 2, 43
        HALFN = CN // 2
        parts = ((0, 4), (4, CW))
        with nc.Block() as block:
            @block.sync
            def _(sp):
                sp.dma_start(gam[:, :], bc(gamma.unsqueeze(0), [P, D])).then_inc(const, 16)
                sp.dma_start(bet[:, :], bc(beta.unsqueeze(0), [P, D])).then_inc(const, 16)
                sp.dma_start(wg[:, :, :], w_gat.rearrange("(c p) n -> p c n", p=P)).then_inc(const, 16)

                def load(i, s):
                    sp.dma_start(xs[s][:, :, :], k.xs_d[bass.ds(i * CN, CN), :].rearrange("(w p) f -> p w f", p=P)).then_inc(landed[s], 16)

                def turn(j, s, first, last):
                    i = j * 2 + s
                    sp.wait_ge(dve, (i + 1) * K)
                    sp.dma_start(k.x2_d[bass.ds(i * CN, CN), :].rearrange("(w p) f -> p w f", p=P), x2[s][:, :, :]).then_inc(stored[s], 16)
                    if not last:
                        load(i + 2, s)
                load(0, 0)
                load(1, 1)
                for i in range(2):
                    turn(0, i, True, False)
                with sp.Fori(1, half - 1) as j:
                    turn(j, 0, False, False)
                    turn(j, 1, False, False)
                turn(half - 1, 0, False, False)
                turn(half - 1, 1, False, True)
                turn(half, 0, False, True)
                for s in range(2):
                    sp.wait_ge(stored[s], 16 * (half + 1 - s))

            @block.vector
            def _(v):
                v.memset(eps[:, :], EPS).then_inc(ready, 1)
                v.wait_ge(const, 48)

                def normalise(ch, src, dst, nth):
                    for w in range(CW):
                        ch.on(v.bn_stats(stats[:, w, :], src[:, w, :]))
                    ch.wait()
                    v.sem_inc(s_stats, 1)
                    for w in range(CW):
                        a = v.bn_aggr(mv[:, w, :], stats[:, w, :])
                    a.then_inc(s_var, 1)
                    v.wait_ge(s_sqrt, nth)
                    ch.on(v.reciprocal(rstd[:, :], rstd[:, :]))
                    ch.wait()
                    for w in range(CW):
                        ch.on(v.tensor_scalar(dst[:, w, :], src[:, w, :], mv[:, w, 0:1], rstd[:, w:w + 1], ALU.subtract, ALU.mult))
                    ch.wait()

                def turn(j, s, first, last):
                    i = j * 2 + s
                    ch = Chain(v, dve, i, K)
                    acc = k.acc[:, bass.ds(i * CW, CW), :].rearrange("p w (h e) -> p w h e", e=HW)
                    v4 = lambda t: t.rearrange("p w (h d) -> p w h d", d=DH)
                    ch.on(v.tensor_scalar(den[:, :, :, :], acc[:, :, :, DH:HW], 1e-30, None, ALU.max))
                    ch.wait()
                    ch.on(v.reciprocal(den[:, :, :, :], den[:, :, :, :]))
                    ch.wait()
                    for w in range(CW):
                        ch.on(v.tensor_tensor(v4(out[:, :, :])[:, w], k.acc[:, bass.ds(i * CW + w, 1), :].rearrange("p a (h e) -> p (a h) e", e=HW)[:, :, 0:DH],
                                              bc(den[:, w, :, :], [P, HEADS, DH]), ALU.mult))
                    ch.wait()
                    v.wait_ge(landed[s], j * 16 + 16)
                    v.tensor_tensor(out[:, :, :], out[:, :, :], xs[s][:, :, D:2 * D], ALU.add).then_inc(s_in, 1)
                    v.wait_ge(s_gelu, i + 1)
                    ch.on(v.tensor_tensor(out[:, :, :], out[:, :, :], xs[s][:, :, 0:D], ALU.add))
                    ch.wait()
                    if not first:
                        v.wait_ge(stored[s], j * 16)
                    normalise(ch, out, x2[s], i * 2 + 1)
                    ch.on(v.tensor_tensor(x2[s][:, :, :], x2[s][:, :, :], bc(gam[:, :].unsqueeze(1), [P, CW, D]), ALU.mult))
                    ch.wait()
                    ch.on(v.tensor_tensor(x2[s][:, :, :], x2[s][:, :, :], bc(bet[:, :].unsqueeze(1), [P, CW, D]), ALU.add))
                    ch.wait()
                    ch.on(v.tensor_tensor(x2[s][:, :, :], x2[s][:, :, :], xs[s][:, :, 2 * D:3 * D], ALU.add))
                    ch.wait()
                    if not (isinstance(i, int) and i == 0):
                        v.wait_ge(turned, i)
                    normalise(ch, x2[s], xn2, i * 2 + 2)
                    ch.done()
                    v.wait_ge(h_ok, i + 1)
                    for q in range(2):
                        r = v.tensor_copy(k.hT[:, bass.ds(i * CN + q * HALFN, HALFN)], h_ps[q][:, 0:HALFN])
                    r.then_inc(h_read, 1)
                pairs(v, half, turn)

            @block.scalar
            def _(act):
                act.wait_ge(ready, 1)

                def root(n):
                    act.wait_ge(s_var, n)
                    act.activation(rstd[:, :], mv[:, :, 1], ACT.Sqrt, bias=eps[:, :]).then_inc(s_sqrt, 1)

                def turn(j, s, first, last):
                    i = j * 2 + s
                    act.wait_ge(s_in, i + 1)
                    act.activation(out[:, :, :], out[:, :, :], ACT.Gelu).then_inc(s_gelu, 1)
                    root(i * 2 + 1)
                    root(i * 2 + 2)
                    act.wait_ge(turned, i + 1)
                    for c in range(2):
                        for q, (a, b) in enumerate(parts):
                            r = act.copy(k.xT[:, c, bass.ds(i * CN + a * P, (b - a) * P)],
                                         turn_ps[2 * c + q][:, 0:b - a, :].rearrange("p w n -> p (w n)"))
                    r.then_inc(xt_ok, 1)
                pairs(act, half, turn)

            @block.tensor
            def _(pe):
                pe.wait_ge(const, 48)

                def turn(j, s, first, last):
                    i = j * 2 + s
                    pe.wait_ge(dve, (i + 1) * K)
                    for c in range(2):
                        for q, (a, b) in enumerate(parts):
                            for w in range(a, b):
                                t = pe.transpose(turn_ps[2 * c + q][:, w - a, :], xn2[:, w, c * P:(c + 1) * P], k.ident[:, :])
                    t.then_inc(turned, 1)
                    pe.wait_ge(xt_ok, i + 1)
                    if not (isinstance(i, int) and i == 0):
                        pe.wait_ge(h_read, i)
                    for q in range(2):
                        for c in range(2):
                            m = pe.matmul(h_ps[q][:, 0:HALFN], wg[:, c, :], k.xT[:, c, bass.ds(i * CN + q * HALFN, HALFN)],
                                          start=(c == 0), stop=(c == 1))
                    m.then_inc(h_ok, 1)
                pairs(pe, half, turn)


def route_tables(nc, k, edge_index, att_src, att_dst):
    with ExitStack() as ctx:
        sb = lambda n, s, d: ctx.enter_context(nc.sbuf_tensor(n, s, d))
        ends = sb("rt_ends", [P, 2, RT], I32)
        dstf = sb("rt_dstf", [P, RT], F32)
        a_idx = sb("rt_a", [P, RT], F32)
        ge = sb("rt_ge", [P, RT], F32)
        iota6 = sb("rt_iota6", [P, BLK], F32)
        att = sb("rt_att", [P, 2, RD], F32)
        tmp = sb("rt_tmp", [P, NW, RD], F32)
        part = sb("rt_part", [P, 1], F32)
        valid = sb("rt_valid", [P, 2], F32)
        masked = sb("rt_masked", [P, NW, RH], F32)
        top = sb("rt_top", [P, 2, RH], F32)
        hn_ps = [ctx.enter_context(nc.psum_tensor(f"rt_h{i}", [P, 32, RD], F32)) for i in range(2)]
        landed, made, dve, turned, top_in, top_ok, tab, stored = (nc.alloc_semaphore(f"rt_{n}") for n in (
            "landed", "constants", "dve", "turned", "max_in", "max", "tables", "stored"))
        with nc.Block() as block:
            @block.sync
            def _(sp):
                sp.dma_start(ends[:, :, :], edge_index.rearrange("a (p c) -> p a c", p=P)).then_inc(landed, 16)
                for i, a in enumerate((att_src, att_dst)):
                    sp.dma_start(att[:, i, :], bc(a.rearrange("h e -> (h e)").unsqueeze(0), [P, RD])).then_inc(landed, 16)
                sp.wait_ge(tab, 1)
                sp.dma_start(k.src_tab_d.rearrange("(w p) f -> p w f", p=P), k.node_src[:, :, :]).then_inc(stored, 16)
                sp.dma_start(k.dst_tab_d.rearrange("(w p) f -> p w f", p=P), k.node_dst[:, :, :]).then_inc(stored, 16)
                sp.wait_ge(stored, 32)

            @block.gpsimd
            def _(pool):
                pool.iota(iota6[:, :], [[1, BLK]], base=0, channel_multiplier=0, allow_small_or_imprecise_dtypes=True).then_inc(made, 1)
                pool.iota(part[:, :], [[0, 1]], base=0, channel_multiplier=1, allow_small_or_imprecise_dtypes=True).then_inc(made, 1)
                pool.iota(k.iota_span[:, :], [[1, 3 * CH]], base=0, channel_multiplier=0, allow_small_or_imprecise_dtypes=True).then_inc(made, 1)
                pool.wait_ge(top_in, 1)
                pool.partition_all_reduce(top[:, 1, :], top[:, 0, :], P, bass.bass_isa.ReduceOp.max).then_inc(top_ok, 1)

            @block.tensor
            def _(pe):
                for w in range(NW):
                    t = pe.transpose(hn_ps[w // 32][:, w % 32, :], k.hT[:, w * P:(w + 1) * P], k.ident[0:RD, 0:RD])
                t.then_inc(turned, 1)

            @block.vector
            def _(v):
                d = Count(dve)
                on = d.on
                wait = lambda: v.wait_ge(dve, d.n)
                v.wait_ge(turned, 1)
                on(v.tensor_copy(k.node_src[:, 0:32, 0:RD], hn_ps[0][:, :, :]))
                on(v.tensor_copy(k.node_src[:, 32:NW, 0:RD], hn_ps[1][:, 0:NW - 32, :]))
                v.wait_ge(landed, 48)
                v.wait_ge(made, 3)
                wait()
                a_src, a_dst = k.node_src[:, :, RD:RV], k.node_dst[:, :, 0:RH]
                for i, a in enumerate((a_src, a_dst)):
                    on(v.tensor_tensor(tmp[:, :, :], k.node_src[:, :, 0:RD], bc(att[:, i:i + 1, :], [P, NW, RD]), ALU.mult))
                    wait()
                    on(v.reduce_sum(a, tmp[:, :, :].rearrange("p w (h e) -> p w h e", e=NE), AX.X))
                    wait()
                on(v.tensor_scalar(valid[:, 0:1], part[:, :], float(TAIL), None, ALU.is_lt))
                wait()
                on(v.tensor_scalar(valid[:, 1:2], valid[:, 0:1], BIG, -BIG, ALU.mult, ALU.add))
                on(v.tensor_copy(masked[:, 0:NW - 1, :], k.node_src[:, 0:NW - 1, RD:RV]))
                wait()
                on(v.tensor_scalar(masked[:, NW - 1, :], k.node_src[:, NW - 1, RD:RV], valid[:, 0:1], valid[:, 1:2], ALU.mult, ALU.add))
                wait()
                v.tensor_reduce(top[:, 0, :], masked[:, :, :].rearrange("p w h -> p h w"), AX.X, ALU.max).then_inc(top_in, 1)
                v.wait_ge(top_ok, 1)
                on(v.tensor_tensor(masked[:, :, :], a_dst, bc(top[:, 1:2, :], [P, NW, RH]), ALU.add))
                wait()
                v.scalar_tensor_tensor(out=k.node_dst[:, :, RH:2 * RH], in0=masked[:, :, :], scalar=0.2, in1=masked[:, :, :],
                                       op0=ALU.mult, op1=ALU.max).then_inc(tab, 1)
                for i in range(2):
                    on(v.tensor_scalar(k.ends[:, :, i, :], ends[:, i, :].rearrange("p (s t) -> p s t", t=RG), float(N - 1), None, ALU.min))
                on(v.tensor_copy(dstf[:, :], ends[:, 1, :]))
                wait()
                on(v.tensor_scalar(a_idx[:, :], dstf[:, :], float(SPAN), None, ALU.is_ge))
                wait()
                for a in range(2, BLK):
                    on(v.tensor_scalar(ge[:, :], dstf[:, :], float(SPAN * a), None, ALU.is_ge))
                    wait()
                    on(v.tensor_tensor(a_idx[:, :], a_idx[:, :], ge[:, :], ALU.add))
                    wait()
                on(v.scalar_tensor_tensor(out=k.column[:, :], in0=a_idx[:, :], scalar=-float(SPAN), in1=dstf[:, :], op0=ALU.mult, op1=ALU.add))
                on(v.tensor_tensor(k.block_oh[:, :, :], bc(a_idx[:, :].unsqueeze(2), [P, RT, BLK]), bc(iota6[:, :].unsqueeze(1), [P, RT, BLK]), ALU.is_equal))
                wait()


def route_edges(nc, k):
    with ExitStack() as ctx:
        sb = lambda n, s, d: ctx.enter_context(nc.sbuf_tensor(n, s, d))
        idx = [sb(f"re_idx{i}", [P, 2 * RG], I32) for i in range(2)]
        gs = [sb(f"re_src{i}", [P, RG, RV], F32) for i in range(2)]
        gd = [sb(f"re_dst{i}", [P, RG, 2 * RH], F32) for i in range(2)]
        e = [sb(f"re_e{i}", [P, RG, RH], F32) for i in range(3)]
        val = sb("re_val", [P, RG, RV], F32)
        rest = sb("re_rest", [P, RG, RV], F32)
        split = [sb(f"re_split{i}", [P, RG, RV], BF16) for i in range(3)]
        spread = [[sb(f"re_spread{i}_{c}", [P, RG, BLK * RV], BF16) for c in range(3)] for i in range(2)]
        col_oh = [sb(f"re_col{t}", [P, 3 * CH], BF16) for t in range(RG)]
        zero = sb("re_zero", [P, 3 * CH], BF16)
        acc = [ctx.enter_context(nc.psum_tensor(f"re_acc{i}", [P, 512], F32)) for i in range(3)]
        names = ("idx", "idx_seen", "dve", "ee", "spread", "column", "tile", "zero", "last")
        ok = {n: nc.alloc_semaphore(f"re_{n}") for n in names}
        landed = [nc.alloc_semaphore(f"re_landed{i}") for i in range(2)]
        K = 8

        def walk(eng, body):
            body(0, 0, True)
            body(0, 1, True)
            with eng.Fori(1, RSTEPS // 2) as j:
                body(j, 0, False)
                body(j, 1, False)

        with nc.Block() as block:
            @block.gpsimd
            def _(pool):

                def gather(j, s, first):
                    i = j * 2 + s
                    if not first:
                        pool.wait_ge(ok["dve"], (i - 2) * K + 4)
                    pool.tensor_copy(idx[s][:, :], k.ends[:, bass.ds(i, 1), :, :].rearrange("p a b t -> p (a b t)")).then_inc(ok["idx"], 1)
                    pool.wait_ge(ok["idx"], i + 1)
                    pool.sem_inc(ok["idx_seen"], 1)
                    for t in range(RG):
                        pool.indirect_dma_start(out=gs[s][:, t, :], out_offset=None, in_=k.src_tab_d,
                                                in_offset=bass.IndirectOffsetOnAxis(ap=idx[s][:, t:t + 1], axis=0)).then_inc(landed[s], 16)
                        pool.indirect_dma_start(out=gd[s][:, t, :], out_offset=None, in_=k.dst_tab_d,
                                                in_offset=bass.IndirectOffsetOnAxis(ap=idx[s][:, RG + t:RG + t + 1], axis=0)).then_inc(landed[s], 16)
                walk(pool, gather)

            @block.scalar
            def _(act):
                def body(j, s, first):
                    i = j * 2 + s
                    act.wait_ge(ok["dve"], i * K + 3)
                    act.activation(val[:, :, RD:RV], e[2][:, :, :], ACT.Exp).then_inc(ok["ee"], 1)
                walk(act, body)

            @block.vector
            def _(v):
                v.memset(zero[:, :], 0.0).then_inc(ok["zero"], 1)

                def body(j, s, first):
                    i = j * 2 + s
                    ch = Chain(v, ok["dve"], i, K)
                    v.wait_ge(landed[s], (j + 1) * (32 * RG))
                    ch.on(v.tensor_tensor(e[0][:, :, :], gs[s][:, :, RD:RV], gd[s][:, :, 0:RH], ALU.add))
                    ch.wait()
                    ch.on(v.scalar_tensor_tensor(out=e[1][:, :, :], in0=e[0][:, :, :], scalar=0.2, in1=e[0][:, :, :], op0=ALU.mult, op1=ALU.max))
                    ch.wait()
                    ch.on(v.tensor_tensor(e[2][:, :, :], e[1][:, :, :], gd[s][:, :, RH:2 * RH], ALU.subtract))
                    ch.wait()
                    v.wait_ge(ok["ee"], i + 1)
                    for t in range(RG):
                        m = v.tensor_tensor(val[:, t, 0:RD].rearrange("p (h e) -> p h e", e=NE), gs[s][:, t, 0:RD].rearrange("p (h e) -> p h e", e=NE),
                                            bc(val[:, t, RD:RV].unsqueeze(2), [P, RH, NE]), ALU.mult)
                    ch.on(m)
                    ch.wait()
                    if not (first and s == 0):
                        v.wait_ge(ok["spread"], i)
                    ch.on(v.tensor_copy(split[0][:, :, :], val[:, :, :]))
                    ch.wait()
                    ch.on(v.tensor_tensor(rest[:, :, :], val[:, :, :], split[0][:, :, :], ALU.subtract))
                    ch.wait()
                    ch.on(v.tensor_copy(split[1][:, :, :], rest[:, :, :]))
                    ch.wait()
                    ch.on(v.tensor_tensor(split[2][:, :, :], rest[:, :, :], split[1][:, :, :], ALU.subtract))
                    ch.wait()
                    if not first:
                        v.wait_ge(ok["tile"], (i - 1) * RG)
                    for c in range(3):
                        for t in range(RG):
                            m = v.tensor_tensor(spread[s][c][:, t, :].rearrange("p (a v) -> p a v", a=BLK),
                                                bc(k.block_oh[:, bass.ds(i * RG + t, 1), :].rearrange("p a b -> p (a b)").unsqueeze(2), [P, BLK, RV]),
                                                bc(split[c][:, t:t + 1, :], [P, BLK, RV]), ALU.mult)
                    m.then_inc(ok["spread"], 1)
                    for t in range(RG):
                        if not (first and s == 0):
                            v.wait_ge(ok["tile"], (i - 1) * RG + t + 1)
                        v.tensor_scalar(col_oh[t][:, :], k.iota_span[:, :], k.column[:, bass.ds(i * RG + t, 1)], None, ALU.is_equal).then_inc(ok["column"], 1)
                walk(v, body)
                v.wait_ge(ok["last"], 1)
                for c in range(3):
                    r = v.tensor_copy(k.sums[:, c * CH:(c + 1) * CH], acc[c][0:BLK * RV, 0:CH])
                r.then_inc(ok["last"], 1)

            @block.tensor
            def _(pe):
                pe.wait_ge(ok["zero"], 1)
                for c in range(3):
                    pe.matmul(acc[c][0:BLK * RV, 0:CH], zero[:, 0:BLK * RV], zero[:, 0:CH], start=True, stop=False)

                def body(j, s, first):
                    i = j * 2 + s
                    pe.wait_ge(ok["spread"], i + 1)
                    for t in range(RG):
                        pe.wait_ge(ok["column"], i * RG + t + 1)
                        for q in range(3):
                            for c in range(3):
                                m = pe.matmul(acc[c][0:BLK * RV, 0:CH], spread[s][q][:, t, :], col_oh[t][:, c * CH:(c + 1) * CH],
                                              start=False, stop=False)
                        m.then_inc(ok["tile"], 1)
                walk(pe, body)
                for c in range(3):
                    m = pe.matmul(acc[c][0:BLK * RV, 0:CH], zero[:, 0:BLK * RV], zero[:, 0:CH], start=False, stop=True)
                m.then_inc(ok["last"], 1)


def route_gates(nc, k, b_gat, ln_gamma, ln_beta):
    with ExitStack() as ctx:
        sb = lambda n, s, d: ctx.enter_context(nc.sbuf_tensor(n, s, d))
        nblk = -(-SPAN // P)
        turned_sb = sb("rg_turned", [P, nblk, BLK * RV], F32)
        r = sb("rg_r", [P, NW, RV], F32)
        con = sb("rg_con", [P, 3, RD], F32)
        t4 = sb("rg_t4", [P, NW, RH], F32)
        u4 = sb("rg_u4", [P, NW, RH], F32)
        s16 = sb("rg_s16", [P, NW, RD], F32)
        u16 = sb("rg_u16", [P, NW, RD], F32)
        one = [sb(f"rg_one{i}", [P, NW, 1], F32) for i in range(4)]
        eps = sb("rg_eps", [P, 1], F32)
        score = sb("rg_score", [P, NW, NE], F32)
        tri = sb("rg_tri", [P, NE, NE], F32)
        bank = [ctx.enter_context(nc.psum_tensor(f"rg_ps{i}", [P, 4, P], F32)) for i in range(3)]
        landed, dve, turned, evac, stored, back, a_in, a_ok = (nc.alloc_semaphore(f"rg_{n}") for n in (
            "landed", "dve", "turned", "evacuated", "stored", "back", "act_in", "act"))
        full = (SPAN // P) * P
        with nc.Block() as block:
            @block.sync
            def _(sp):
                for i, a in enumerate((b_gat, ln_gamma, ln_beta)):
                    sp.dma_start(con[:, i, :], bc(a.unsqueeze(0), [P, RD])).then_inc(landed, 16)
                sp.wait_ge(evac, 4)
                for a in range(BLK):
                    cols = slice(a * RV, (a + 1) * RV)
                    sp.dma_start(k.sums_d[a * SPAN:a * SPAN + full, :].rearrange("(k p) f -> p k f", p=P), turned_sb[:, 0:full // P, cols]).then_inc(stored, 16)
                    sp.dma_start(k.sums_d[a * SPAN + full:(a + 1) * SPAN, :], turned_sb[0:SPAN - full, full // P, cols]).then_inc(stored, 16)
                sp.wait_ge(stored, 32 * BLK)
                sp.dma_start(r[:, 0:NW - 1, :], k.sums_d[0:(NW - 1) * P, :].rearrange("(w p) f -> p w f", p=P)).then_inc(back, 16)
                sp.dma_start(r[0:TAIL, NW - 1, :], k.sums_d[(NW - 1) * P:N, :]).then_inc(back, 16)

            @block.tensor
            def _(pe):
                for b in range(nblk):
                    n = min(P, 3 * CH - b * P)
                    t = pe.transpose(bank[b // 4][0:n, b % 4, 0:BLK * RV], k.sums[:, b * P:b * P + n], k.ident[0:BLK * RV, 0:BLK * RV])
                t.then_inc(turned, 1)

            @block.scalar
            def _(act):
                def step(n, out, in_, f, **kw):
                    act.wait_ge(a_in, n)
                    act.activation(out, in_, f, **kw).then_inc(a_ok, 1)
                step(1, u4[:, :, :], t4[:, :, :], ACT.Exp)
                step(2, one[2][:, :, :], one[1][:, :, :], ACT.Sqrt, bias=eps[:, :])
                step(3, u4[:, :, :], t4[:, :, :], ACT.Exp)

            @block.vector
            def _(v):
                d = Count(dve)
                wait = lambda: v.wait_ge(dve, d.n)

                def on(ins):
                    d.on(ins)
                    wait()

                def tt(o, a, b, op):
                    on(v.tensor_tensor(o, a, b, op))
                on(v.memset(eps[:, :], EPS))
                on(v.memset(tri[:, :, :], 0.0))
                for i in range(1, NE):
                    on(v.memset(tri[:, i, 0:i], 1.0))
                v.memset(r[:, NW - 1, :], 1.0).then_inc(evac, 1)
                v.wait_ge(turned, 1)
                for b in range(3):
                    w = (4, 4, nblk - 8)[b]
                    n = P if b < 2 else 3 * CH - 8 * P
                    v.tensor_copy(turned_sb[0:n, 4 * b:4 * b + w, :], bank[b][0:n, 0:w, 0:BLK * RV]).then_inc(evac, 1)
                full16, full4 = [P, NW, RD], [P, NW, RH]
                he = lambda t: t.rearrange("p w (h e) -> p (w h) e", e=NE)
                flat = lambda t: t.rearrange("p w h -> p (w h)").unsqueeze(2)
                h, a_src = k.node_src[:, :, 0:RD], k.node_src[:, :, RD:RV]
                tt(u4[:, :, :], a_src, k.node_dst[:, :, 0:RH], ALU.add)
                on(v.scalar_tensor_tensor(out=t4[:, :, :], in0=u4[:, :, :], scalar=0.2, in1=u4[:, :, :], op0=ALU.mult, op1=ALU.max))
                tt(t4[:, :, :], t4[:, :, :], k.node_dst[:, :, RH:2 * RH], ALU.subtract)
                v.sem_inc(a_in, 1)
                v.wait_ge(a_ok, 1)
                on(v.tensor_copy(s16[:, :, :], h))
                tt(he(s16[:, :, :]), he(s16[:, :, :]), bc(flat(u4[:, :, :]), [P, NW * RH, NE]), ALU.mult)
                v.wait_ge(back, 32)
                tt(s16[:, :, :], s16[:, :, :], r[:, :, 0:RD], ALU.add)
                tt(t4[:, :, :], u4[:, :, :], r[:, :, RD:RV], ALU.add)
                on(v.tensor_scalar(t4[:, :, :], t4[:, :, :], 1e-16, None, ALU.add))
                on(v.reciprocal(u4[:, :, :], t4[:, :, :]))
                tt(he(s16[:, :, :]), he(s16[:, :, :]), bc(flat(u4[:, :, :]), [P, NW * RH, NE]), ALU.mult)
                v.wait_ge(landed, 48)
                tt(s16[:, :, :], s16[:, :, :], bc(con[:, 0:1, :], full16), ALU.add)
                on(v.reduce_sum(one[0][:, :, :], s16[:, :, :], AX.X))
                on(v.tensor_scalar(one[0][:, :, :], one[0][:, :, :], 1.0 / RD, None, ALU.mult))
                tt(s16[:, :, :], s16[:, :, :], bc(one[0][:, :, :], full16), ALU.subtract)
                tt(u16[:, :, :], s16[:, :, :], s16[:, :, :], ALU.mult)
                on(v.reduce_sum(one[1][:, :, :], u16[:, :, :], AX.X))
                on(v.tensor_scalar(one[1][:, :, :], one[1][:, :, :], 1.0 / RD, None, ALU.mult))
                v.sem_inc(a_in, 1)
                v.wait_ge(a_ok, 2)
                on(v.reciprocal(one[3][:, :, :], one[2][:, :, :]))
                tt(s16[:, :, :], s16[:, :, :], bc(one[3][:, :, :], full16), ALU.mult)
                tt(s16[:, :, :], s16[:, :, :], bc(con[:, 1:2, :], full16), ALU.mult)
                tt(s16[:, :, :], s16[:, :, :], bc(con[:, 2:3, :], full16), ALU.add)
                on(v.reduce_sum(score[:, :, :], s16[:, :, :].rearrange("p w (h e) -> p w e h", e=NE), AX.X))
                on(v.tensor_scalar(score[:, :, :], score[:, :, :], 1.0 / RH, None, ALU.mult))
                on(v.memset(t4[:, :, :], 0.0))
                for j in range(NE):
                    sj = bc(score[:, :, j:j + 1], full4)
                    tt(u4[:, :, :], sj, score[:, :, :], ALU.is_gt)
                    tt(t4[:, :, :], t4[:, :, :], u4[:, :, :], ALU.add)
                    tt(u4[:, :, :], sj, score[:, :, :], ALU.is_equal)
                    tt(u4[:, :, :], u4[:, :, :], bc(tri[:, :, j].unsqueeze(1), full4), ALU.mult)
                    tt(t4[:, :, :], t4[:, :, :], u4[:, :, :], ALU.add)
                on(v.tensor_scalar(s16[:, :, 0:NE], t4[:, :, :], 1.5, None, ALU.is_lt))
                on(v.tensor_reduce(one[0][:, :, :], score[:, :, :], AX.X, ALU.max))
                tt(t4[:, :, :], score[:, :, :], bc(one[0][:, :, :], full4), ALU.subtract)
                v.sem_inc(a_in, 1)
                v.wait_ge(a_ok, 3)
                tt(u4[:, :, :], u4[:, :, :], s16[:, :, 0:NE], ALU.mult)
                on(v.reduce_sum(one[1][:, :, :], u4[:, :, :], AX.X))
                on(v.reciprocal(one[2][:, :, :], one[1][:, :, :]))
                tt(k.gates[:, :, :], u4[:, :, :], bc(one[2][:, :, :], full4), ALU.mult)


def experts(nc, k, w1, b1, w2, b2, out):
    with ExitStack() as ctx:
        sb = lambda n, s, d: ctx.enter_context(nc.sbuf_tensor(n, s, d))
        FT = FF // P
        w1_sb = sb("ex_w1", [P, NE, 2, FF], F32)
        w2_sb = sb("ex_w2", [P, NE, FT, D], F32)
        b1_sb = sb("ex_b1", [P, NE, FT], F32)
        b2_sb = sb("ex_b2", [P, NE, D], F32)
        hid = [sb(f"ex_hid{i}", [P, FT, CN], F32) for i in range(2)]
        o = [sb(f"ex_o{i}", [P, CW, D], F32) for i in range(2)]
        h_ps = [ctx.enter_context(nc.psum_tensor(f"ex_h{i}", [P, 512], F32)) for i in range(4)]
        y_ps = [ctx.enter_context(nc.psum_tensor(f"ex_y{i}", [P, 512], F32)) for i in range(4)]
        landed, h_ok, gelu, y_ok, added, biased = (nc.alloc_semaphore(f"ex_{n}") for n in ("landed", "h", "gelu", "y", "added", "biased"))
        x_in = [nc.alloc_semaphore(f"ex_x{i}") for i in range(2)]
        stored = [nc.alloc_semaphore(f"ex_stored{i}") for i in range(2)]
        half, HALFN = NB // 2, CN // 2
        HT = 2 * FT
        YT = CW
        with nc.Block() as block:
            @block.sync
            def _(sp):
                sp.dma_start(w1_sb[:, :, :, :], w1.rearrange("e (c p) n -> p e c n", p=P)).then_inc(landed, 16)
                sp.dma_start(w2_sb[:, :, :, :], w2.rearrange("e (f p) n -> p e f n", p=P)).then_inc(landed, 16)
                sp.dma_start(b1_sb[:, :, :], b1.rearrange("e (f p) -> p e f", p=P), allow_slow_non_contiguous=True).then_inc(landed, 16)
                sp.dma_start(b2_sb[:, :, :], bc(b2.unsqueeze(0), [P, NE, D])).then_inc(landed, 16)

                def load(i, s):
                    sp.dma_start(o[s][:, :, :], k.x2_d[bass.ds(i * CN, CN), :].rearrange("(w p) f -> p w f", p=P)).then_inc(x_in[s], 16)

                def turn(j, s, load_next, last=False):
                    i = j * 2 + s
                    sp.wait_ge(added, (i + 1) * (NE * YT))
                    if last:
                        sp.dma_start(out[(NB - 1) * CN:(NW - 1) * P, :].rearrange("(w p) f -> p w f", p=P), o[s][:, 0:CW - 1, :]).then_inc(stored[s], 16)
                        sp.dma_start(out[(NW - 1) * P:N, :], o[s][0:TAIL, CW - 1, :]).then_inc(stored[s], 16)
                    else:
                        sp.dma_start(out[bass.ds(i * CN, CN), :].rearrange("(w p) f -> p w f", p=P), o[s][:, :, :]).then_inc(stored[s], 16)
                        if load_next:
                            sp.wait_ge(stored[s], (j + 1) * 16)
                            load(i + 2, s)
                load(0, 0)
                load(1, 1)
                with sp.Fori(0, half - 1) as j:
                    turn(j, 0, True)
                    turn(j, 1, True)
                turn(half - 1, 0, True)
                turn(half - 1, 1, False)
                turn(half, 0, False, True)
                sp.wait_ge(stored[0], 16 * (half + 2))
                sp.wait_ge(stored[1], 16 * half)

            @block.tensor
            def _(pe):
                pe.wait_ge(landed, 64)

                def hidden(i, e, first):
                    u = i * NE + e
                    for f in range(FT):
                        for q in range(2):
                            n = f * 2 + q
                            if not first or n >= 4:
                                pe.wait_ge(gelu, u * HT + (n - 3))
                            for c in range(2):
                                m = pe.matmul(h_ps[n % 4][:, 0:HALFN], w1_sb[:, e, c, f * P:(f + 1) * P],
                                              k.xT[:, c, bass.ds(i * CN + q * HALFN, HALFN)], start=(c == 0), stop=(c == 1))
                            m.then_inc(h_ok, 1)

                def turn(j, s, first, last):
                    i = j * 2 + s
                    for e in range(NE):
                        if e + 1 < NE:
                            hidden(i, e + 1, False)
                        elif not last:
                            hidden(i + 1, 0, False)
                        u = i * NE + e
                        pe.wait_ge(gelu, (u + 1) * HT)
                        for w in range(CW):
                            n = e * YT + w
                            if not (first and s == 0 and n < 4):
                                pe.wait_ge(added, i * (NE * YT) + (n - 3))
                            for f in range(FT):
                                m = pe.matmul(y_ps[n % 4][:, 0:D], hid[e % 2][:, f, w * P:(w + 1) * P], w2_sb[:, e, f, :],
                                              start=(f == 0), stop=(f == FT - 1))
                            m.then_inc(y_ok, 1)
                hidden(0, 0, True)
                pairs(pe, half, turn)

            @block.scalar
            def _(act):
                act.wait_ge(landed, 64)

                def turn(j, s, first, last):
                    i = j * 2 + s
                    for e in range(NE):
                        u = i * NE + e
                        if not (first and s == 0 and e < 2):
                            act.wait_ge(y_ok, (u - 1) * YT)
                        for n in range(HT):
                            f, q = n // 2, n % 2
                            act.wait_ge(h_ok, u * HT + n + 1)
                            act.activation(hid[e % 2][:, f, q * HALFN:(q + 1) * HALFN], h_ps[n % 4][:, 0:HALFN], ACT.Gelu,
                                           bias=b1_sb[:, e, f:f + 1]).then_inc(gelu, 1)
                pairs(act, half, turn)

            @block.vector
            def _(v):
                v.wait_ge(landed, 64)

                def turn(j, s, first, last):
                    i = j * 2 + s
                    gate = lambda w, e: k.gates[:, bass.ds(i * CW + w, 1), e:e + 1].rearrange("p a b -> p (a b)")
                    v.wait_ge(x_in[s], (j + 1) * 16)
                    for e in range(NE):
                        if not (first and s == 0 and e == 0):
                            v.wait_ge(biased, (i * NE + e) * CW)
                        for w in range(CW):
                            v.scalar_tensor_tensor(out=o[s][:, w, :], in0=b2_sb[:, e, :], scalar=gate(w, e), in1=o[s][:, w, :],
                                                   op0=ALU.mult, op1=ALU.add).then_inc(biased, 1)
                    v.wait_ge(biased, (i + 1) * (NE * CW))
                    for e in range(NE):
                        for w in range(CW):
                            n = e * YT + w
                            v.wait_ge(y_ok, i * (NE * YT) + n + 1)
                            if e:
                                v.wait_ge(added, i * (NE * YT) + (n - YT + 1))
                            v.scalar_tensor_tensor(out=o[s][:, w, :], in0=y_ps[n % 4][:, 0:D], scalar=gate(w, e), in1=o[s][:, w, :],
                                                   op0=ALU.mult, op1=ALU.add).then_inc(added, 1)
                pairs(v, half, turn)


class Store:
    pass


def graph_layers(nc, x, src, dst, Wq, bq, Wk, bk, Wv, bv, Wskip, bskip, gamma, beta,
                 W_gat, att_src, att_dst, b_gat, ln_gamma, ln_beta, W1, b1, W2, b2, edge_index, out):
    k = Store()
    dram = lambda n, s: nc.dram_tensor(n, s, F32).ap()
    k.reset_d = dram("reset_d", (KROW * P, HEADS, P))
    k.kv_d = dram("kv_d", (NPAD, 2 * D))
    k.xs_d = dram("xs_d", (NPAD, 3 * D))
    k.q3_d = nc.dram_tensor("q3_d", (NPAD, 3 * D), BF16).ap()
    k.x2_d = dram("x2_d", (NPAD, D))
    k.src_tab_d = dram("src_tab_d", (NPAD, RV))
    k.dst_tab_d = dram("dst_tab_d", (NPAD, 2 * RH))
    k.sums_d = dram("sums_d", (BLK * SPAN, RV))
    with ExitStack() as whole:
        sb = lambda ctx, n, s, d: ctx.enter_context(nc.sbuf_tensor(n, s, d))
        k.ident = sb(whole, "ident", [P, P], F32)
        k.gates = sb(whole, "gates", [P, NW, NE], F32)
        k.acc = sb(whole, "acc", [P, NW, HEADS * HW], F32)
        with ExitStack() as walk:
            k.ident_b = sb(walk, "ident_b", [P, P], BF16)
            k.negbig = sb(walk, "negbig", [P, HEADS], BF16)
            k.ones_b = sb(walk, "ones_b", [P, P], BF16)
            k.iota_b = sb(walk, "iota_b", [P, P], BF16)
            k.one = sb(walk, "one", [P, 1], F32)
            k.src_i = sb(walk, "src_i", [P, NT], I32)
            k.dst_f = sb(walk, "dst_f", [P, NT], F32)
            k.last_b = sb(walk, "last_b", [P, NT], BF16)
            k.wbase = sb(walk, "wbase", [P, NS], F32)
            k.w_tab = sb(walk, "w_tab", [1, NS], I32)
            k.g_tab = sb(walk, "g_tab", [1, NS], I32)
            k.m_all = sb(walk, "m_all", [P, NW, HEADS], F32)
            edge_tables(nc, k, src, dst)
            project(nc, k, x, (Wk, Wv, Wq, Wskip), (bk, bv, bq, bskip))
            attend(nc, k)
        k.xT = sb(whole, "xT", [P, 2, NPAD], F32)
        with ExitStack() as route:
            k.node_src = sb(route, "node_src", [P, NW, RV], F32)
            k.node_dst = sb(route, "node_dst", [P, NW, 2 * RH], F32)
            with ExitStack() as ctx:
                k.hT = sb(ctx, "hT", [RD, NPAD], F32)
                node_update(nc, k, gamma, beta, W_gat)
                k.ends = sb(ctx, "route_ends", [P, RSTEPS, 2, RG], I32)
                k.column = sb(ctx, "column", [P, RT], F32)
                k.block_oh = sb(ctx, "block_oh", [P, RT, BLK], BF16)
                k.iota_span = sb(ctx, "iota_span", [P, 3 * CH], F16)
                k.sums = sb(ctx, "sums", [BLK * RV, 3 * CH], F32)
                route_tables(nc, k, edge_index, att_src, att_dst)
                route_edges(nc, k)
                route_gates(nc, k, b_gat, ln_gamma, ln_beta)
        experts(nc, k, W1, b1, W2, b2, out)


_INS = ["x", "src", "dst"] + ["L0_gnn_" + n for n in ("Wq", "bq", "Wk", "bk", "Wv", "bv", "Wskip", "bskip", "gamma", "beta")] \
    + ["L0_ffn_" + n for n in ("W_gat", "att_src", "att_dst", "b_gat", "ln_gamma", "ln_beta", "W1", "b1", "W2", "b2", "edge_index")]


def kernel(**inputs):
    import numpy as _np
    import concourse.bacc as _bacc
    from concourse.bass_utils import run_bass_kernel_spmd as _run

    nc = _bacc.Bacc("TRN2", target_bir_lowering=False, num_devices=1)
    arrays, args = {}, []
    for name in _INS:
        a = _np.ascontiguousarray(inputs[name])
        arrays[f"in_{name}_dram"] = a
        args.append(nc.dram_tensor(f"in_{name}_dram", a.shape, mybir.dt.from_np(a.dtype), kind="ExternalInput").ap())
    args.append(nc.dram_tensor("out_0_dram", (N, D), F32, kind="ExternalOutput").ap())
    graph_layers(nc, *args)
    r = _run(nc, [arrays], core_ids=[0])
    return r.results[0]["out_0_dram"]
```
